# Optimizing a Trainium2 kernel written in Bass

```python
import numpy as np
import jax
import jax.numpy as jnp

def _softmax(x, axis=-1):
    return jax.nn.softmax(x, axis=axis)

def _gelu(x):
    return jax.nn.gelu(x, approximate=True)

def _silu(x):
    return jax.nn.silu(x)

def _sigmoid(x):
    return jax.nn.sigmoid(x)

def _layernorm(x, axis=-1, eps=1e-05):
    m = jnp.mean(x, axis=axis, keepdims=True)
    v = jnp.var(x, axis=axis, keepdims=True)
    return (x - m) / jnp.sqrt(v + eps)

def _scatter_add(tgt, idx, src, axis=0):
    return tgt.at[idx].add(src)

def _segment_sum(src, seg, n):
    return jax.ops.segment_sum(src, seg, n)
kernel_name = 'mk_gnn_preln_d2_gnn_r8_4cfd62'

def setup_inputs(seed: int=0):
    np.random.seed(seed)
    _w = jnp.asarray

    def _rec_inputs():
        import jax
        import jax.numpy as jnp
        _gk = jax.random.key(seed)
        x = -0.0003713 + 1 * jax.random.normal(jax.random.fold_in(_gk, 1), (6250, 128), jnp.float32)
        src = jax.random.randint(jax.random.fold_in(_gk, 2), (200000,), 0, 6250, jnp.int32)
        dst = jnp.minimum((6250 * jax.random.uniform(jax.random.fold_in(_gk, 3), (200000,)) ** 2.0).astype(jnp.int32), 49999)
        _o = jnp.argsort(dst, stable=True)
        src = src[_o]
        dst = dst[_o]
        edge_attr_64 = 0.000102155 + 1.00015 * jax.random.normal(jax.random.fold_in(_gk, 11), (200000, 64), jnp.float32)
        edge_weight = jax.random.uniform(jax.random.fold_in(_gk, 13), (200000,), jnp.float32, 0.0, 0.999999)
        return (x, src, dst, edge_attr_64, edge_weight)
    x, src, dst, edge_attr_64, edge_weight = _rec_inputs()

    def _L0_gnn_setup():
        import jax, jax.numpy as jnp
        import numpy as np
        N_NODES = 12500
        N_EDGES = 62500
        IN_CH = 128
        EDGE_CH = 64

        def _glorot(key, shape):
            fan_in, fan_out = (shape[0], shape[1])
            lim = (6.0 / (fan_in + fan_out)) ** 0.5
            return jax.random.uniform(key, shape, jnp.float32, -lim, lim)
        key = jax.random.key(seed)
        ks = jax.random.split(key, 14)
        x = jax.random.normal(ks[0], (N_NODES, IN_CH), jnp.float32)
        edge_index = jax.random.randint(ks[1], (2, N_EDGES), 0, N_NODES, jnp.int64)
        edge_attr = jax.random.normal(ks[2], (N_EDGES, EDGE_CH), jnp.float32)
        timestamps = jax.random.uniform(ks[3], (N_EDGES,), jnp.float32)
        We1 = _glorot(ks[4], (EDGE_CH, 2 * EDGE_CH))
        be1 = jnp.zeros((2 * EDGE_CH,), jnp.float32)
        We2 = _glorot(ks[5], (2 * EDGE_CH, IN_CH))
        be2 = jnp.zeros((IN_CH,), jnp.float32)
        Wt = _glorot(ks[6], (1, IN_CH))
        bt = jnp.zeros((IN_CH,), jnp.float32)
        Wn1 = _glorot(ks[7], (2 * IN_CH, IN_CH))
        bn1 = jnp.zeros((IN_CH,), jnp.float32)
        Wn2 = _glorot(ks[8], (IN_CH, IN_CH))
        bn2 = jnp.zeros((IN_CH,), jnp.float32)
        return {'x': x, 'edge_index': edge_index, 'edge_attr': edge_attr, 'timestamps': timestamps, 'We1': We1, 'be1': be1, 'We2': We2, 'be2': be2, 'Wt': Wt, 'bt': bt, 'Wn1': Wn1, 'bn1': bn1, 'Wn2': Wn2, 'bn2': bn2}
    _L0_gnn_all = _L0_gnn_setup()
    _L0_gnn_in = {k: v for k, v in _L0_gnn_all.items() if k in ('We1', 'be1', 'We2', 'be2', 'Wt', 'bt', 'Wn1', 'bn1', 'Wn2', 'bn2')}
    del _L0_gnn_all

    def _L1_gnn_setup():
        import jax, jax.numpy as jnp
        import numpy as np
        N_NODES = 6250
        key = jax.random.key(seed)
        ks = jax.random.split(key, 5)
        d_in, d_out = (128, 128)
        x = jax.random.normal(ks[0], (N_NODES, d_in), dtype=jnp.float32)
        edge_index = jax.random.randint(ks[1], (2, 100000), 0, N_NODES, dtype=jnp.int64)
        W1 = jax.random.normal(ks[2], (d_in, d_out), dtype=jnp.float32) * (1.0 / np.sqrt(d_in))
        b1 = jnp.zeros((d_out,), dtype=jnp.float32)
        W2 = jax.random.normal(ks[3], (d_out, d_out), dtype=jnp.float32) * (1.0 / np.sqrt(d_out))
        b2 = jnp.zeros((d_out,), dtype=jnp.float32)
        return {'x': x, 'edge_index': edge_index, 'W1': W1, 'b1': b1, 'W2': W2, 'b2': b2}
    _L1_gnn_all = _L1_gnn_setup()
    _L1_gnn_in = {k: v for k, v in _L1_gnn_all.items() if k in ('W1', 'b1', 'W2', 'b2')}
    del _L1_gnn_all
    return {'x': x, 'src': src, 'dst': dst, 'edge_attr_64': edge_attr_64, 'edge_weight': edge_weight, 'L0_gnn_We1': _L0_gnn_in['We1'], 'L0_gnn_be1': _L0_gnn_in['be1'], 'L0_gnn_We2': _L0_gnn_in['We2'], 'L0_gnn_be2': _L0_gnn_in['be2'], 'L0_gnn_Wt': _L0_gnn_in['Wt'], 'L0_gnn_bt': _L0_gnn_in['bt'], 'L0_gnn_Wn1': _L0_gnn_in['Wn1'], 'L0_gnn_bn1': _L0_gnn_in['bn1'], 'L0_gnn_Wn2': _L0_gnn_in['Wn2'], 'L0_gnn_bn2': _L0_gnn_in['bn2'], 'L1_gnn_W1': _L1_gnn_in['W1'], 'L1_gnn_b1': _L1_gnn_in['b1'], 'L1_gnn_W2': _L1_gnn_in['W2'], 'L1_gnn_b2': _L1_gnn_in['b2']}

def reference(x, src, dst, edge_attr_64, edge_weight, L0_gnn_We1, L0_gnn_be1, L0_gnn_We2, L0_gnn_be2, L0_gnn_Wt, L0_gnn_bt, L0_gnn_Wn1, L0_gnn_bn1, L0_gnn_Wn2, L0_gnn_bn2, L1_gnn_W1, L1_gnn_b1, L1_gnn_W2, L1_gnn_b2):
    import jax
    import jax.numpy as jnp

    def _L0_gnn_ref(x, edge_index, edge_attr, timestamps, We1, be1, We2, be2, Wt, bt, Wn1, bn1, Wn2, bn2):
        import jax, jax.numpy as jnp
        import numpy as np
        N_NODES = 12500
        N_EDGES = 62500
        IN_CH = 128
        EDGE_CH = 64

        def _glorot(key, shape):
            fan_in, fan_out = (shape[0], shape[1])
            lim = (6.0 / (fan_in + fan_out)) ** 0.5
            return jax.random.uniform(key, shape, jnp.float32, -lim, lim)
        ts = timestamps[:, None]
        ef = jax.nn.relu(edge_attr @ We1 + be1) @ We2 + be2
        tw = jax.nn.sigmoid(ts @ Wt + bt)
        ef = ef * tw
        row, col = (edge_index[0], edge_index[1])
        combined = jnp.concatenate([x[row], ef], axis=1)
        msg = jax.nn.relu(combined @ Wn1 + bn1) @ Wn2 + bn2
        out = jax.ops.segment_sum(msg, col, num_segments=x.shape[0])
        return out + x

    def _L1_gnn_ref(x, edge_index, W1, b1, W2, b2):
        import jax, jax.numpy as jnp
        import numpy as np
        N_NODES = 6250
        src, dst = (edge_index[0], edge_index[1])
        agg = jax.ops.segment_sum(x[src], dst, num_segments=x.shape[0])
        h = x + agg
        h = jax.nn.relu(h @ W1 + b1)
        h = h @ W2 + b2
        return jax.nn.relu(h)
    edge_index = jnp.stack([src, dst])
    h = jnp.maximum(_layernorm(x, axis=-1), 0.0)
    x = x + _L0_gnn_ref(h, edge_index, edge_attr_64, edge_weight, L0_gnn_We1, L0_gnn_be1, L0_gnn_We2, L0_gnn_be2, L0_gnn_Wt, L0_gnn_bt, L0_gnn_Wn1, L0_gnn_bn1, L0_gnn_Wn2, L0_gnn_bn2)
    h = jnp.maximum(_layernorm(x, axis=-1), 0.0)
    x = x + _L1_gnn_ref(h, edge_index, L1_gnn_W1, L1_gnn_b1, L1_gnn_W2, L1_gnn_b2)
    return x

_drawn_inputs = setup_inputs


def setup_inputs(seed=0):
    import zlib

    import numpy as np

    out = dict(_drawn_inputs(seed))
    spreads = {'L0_gnn_be1': (0.0, 0.1),
     'L0_gnn_be2': (0.0, 0.1),
     'L0_gnn_bt': (0.0, 0.65),
     'L0_gnn_bn1': (0.0, 0.1),
     'L0_gnn_bn2': (0.0, 0.1),
     'L1_gnn_b1': (0.0, 2.0),
     'L1_gnn_b2': (0.0, 2.0)}
    factors = {'edge_weight': 45.774, 'L0_gnn_Wt': 7.198}
    for name, (base, spread) in spreads.items():
        noise = np.random.default_rng([zlib.crc32(name.encode()), seed]).standard_normal(out[name].shape)
        drawn = base * np.exp(spread * noise) if base else spread * noise
        out[name] = jnp.asarray(drawn.astype(out[name].dtype))
    for name, factor in factors.items():
        out[name] = (out[name] * factor).astype(out[name].dtype)
    return out
```

```python
from contextlib import ExitStack

import concourse.bass as bass
from concourse import mybir

F32 = mybir.dt.float32
F32R = mybir.dt.float32r
BF16 = mybir.dt.bfloat16
I32 = mybir.dt.int32
ALU = mybir.AluOpType
ACT = mybir.ActivationFunctionType
AX = mybir.AxisListType

P = 128
D = 128
K_EDGE = 64
N_NODES = 6250
N_EDGES = 200000
EPS = 1e-5

NT = -(-N_NODES // P)
GT = 7
NG = NT // GT
N_PAD = NT * P
assert NG * GT == NT

TB = 4
BLK = TB * P
RING = 4
NPAIR = -(-N_EDGES // (2 * BLK * RING)) * RING
NBODY = NPAIR // RING
NB = 2 * NPAIR
NTILE = NB * TB
E_PAD = NTILE * P

W_LOG2 = 6
W = 1 << W_LOG2
ACC = N_PAD + W
NBP = 98
NBJ = NB // NBP
assert NBP * NBJ == NB
MAX_SWEEPS = N_PAD // W + 1
FULL_TILES = N_EDGES // P
TAIL = N_EDGES % P
assert TAIL in (0, 32, 64, 96)
NP3 = 3
ZK = NP3 * NP3


def gnn_program(nc, x, ea, ew, src, dst_tiles, dst_blocks, We1, be1, We2, be2, Wt, bt, Wn1, bn1, Wn2, bn2,
                W1, b1, W2, b2, out):
    ctx = ExitStack()
    with ctx:
        def sb(name, shape, dt=F32):
            return ctx.enter_context(nc.sbuf_tensor(name, shape, dt))

        def sem(name):
            return ctx.enter_context(nc.semaphore(name))

        def dram(name, shape, dt=F32):
            return nc.dram_tensor(name, shape, dt, kind="Internal").ap()

        table0 = dram("table0", (N_PAD, D))
        table1 = dram("table1", (N_PAD, D))
        ew_rows = dram("ew_rows", (ZK, E_PAD), BF16)
        base_d = dram("base_d", (NB,), I32)
        span_d = dram("span_d", (NB,), I32)

        xs = sb("xs", [P, NT, D])
        nodes = sb("nodes", [P, NT, D])
        acc = sb("acc", [P, 2, ACC])
        stats = sb("stats", [P, NT, 6])
        mean = sb("mean", [P, NT])
        half = sb("half", [P, NT])
        var = sb("var", [P, NT])
        rstd = sb("rstd", [P, NT])
        shift = sb("shift", [P, NT])
        count_n = sb("count_n", [P, NT])
        stage = sb("stage", [P, GT, D])
        stage2 = sb("stage2", [P, GT, D])

        we1 = sb("we1", [P, D])
        we2 = sb("we2", [P, D])
        wn1a = sb("wn1a", [P, D])
        wn1b = sb("wn1b", [P, D])
        wn2 = sb("wn2", [P, D])
        w1 = sb("w1", [P, D])
        w2 = sb("w2", [P, D])
        cols = sb("cols", [P, 4])
        be1_c, be2_c, bt_c, b1_c = (cols[:, i:i + 1] for i in range(4))
        bn1_r = sb("bn1_r", [P, D])
        bn2_r = sb("bn2_r", [P, D])
        b2_r = sb("b2_r", [P, D])
        wt_f = sb("wt_f", [ZK, D])
        wt_p = sb("wt_p", [ZK, NP3, D], BF16)
        wt9 = sb("wt9", [ZK, D], BF16)
        ones = sb("ones", [P, P], F32R)
        iota_s = sb("iota_s", [P, W])

        ew_f = sb("ew_f", [P, E_PAD // P])
        ew_p = sb("ew_p", [P, NP3, E_PAD // P], BF16)
        dst_t = sb("dst_t", [P, NTILE], I32)
        dst_b = sb("dst_b", [NBP, NBJ, BLK], I32)
        least = sb("least", [NBP, NBJ], I32)
        span = sb("span", [NBP, NBJ], I32)
        base_first = sb("base_first", [1, NB], I32)
        base_now = sb("base_now", [1, NB], I32)
        base_all = sb("base_all", [P, NB], I32)
        span_row = sb("span_row", [1, NB], I32)
        sweeps_s = sb("sweeps_s", [1, 1], I32)
        rel = sb("rel", [P, NTILE])
        ea_s = sb("ea_s", [P, RING, BLK])
        ew_s = sb("ew_s", [ZK, RING, 2, BLK], BF16)
        idx = sb("idx", [P, RING, 2 * TB], I32)
        rows = sb("rows", [P, RING, 2, TB, D])
        hid = sb("hid", [P, 2, BLK])
        tw = sb("tw", [P, 2, BLK])
        ef = sb("ef", [P, 2, BLK])
        msg = sb("msg", [P, 2, TB, D])
        hot = sb("hot", [P, 2, TB, W], F32R)

        BANK = 512
        ps = ctx.enter_context(nc.psum_tensor("ps", [P, 8 * BANK], F32))
        p_hid = [ps[:, q * BANK:(q + 1) * BANK] for q in (0, 1)]
        p_z = ps[:, 2 * BANK:3 * BANK]
        p_ef = [ps[:, q * BANK:(q + 1) * BANK] for q in (3, 4)]
        p_pre = [ps[:, q * BANK:(q + 1) * BANK] for q in (5, 6)]
        p_agg = ps[:, 7 * BANK:7 * BANK + 4 * W].rearrange("p (q s w) -> p q s w", q=2, s=2)
        p_iota = ps[:, 7 * BANK + 4 * W:7 * BANK + 5 * W]
        p_turn = ps[:, 0:GT * D].rearrange("p (t d) -> p t d", t=GT)
        p_prod = ps[:, 2 * BANK:2 * BANK + GT * D].rearrange("p (t d) -> p t d", t=GT)

        ident = sb("ident", [P, P])

        x_loaded = [sem(f"x_loaded{g}") for g in range(NG)]
        params_loaded = sem("params_loaded")
        dst_loaded = sem("dst_loaded")
        ew_loaded = sem("ew_loaded")
        consts_made = sem("consts_made")
        base_made = sem("base_made")
        base_stored = sem("base_stored")
        base_loaded = sem("base_loaded")
        sweeps_made = sem("sweeps_made")
        ew_split = sem("ew_split")
        ew_stored = sem("ew_stored")
        wt_placed = sem("wt_placed")
        dve_chain = sem("dve_chain")
        var_made = sem("var_made")
        root_made = sem("root_made")
        stats_made = sem("stats_made")
        normed = sem("normed")
        turned = sem("turned")
        stage2_made = sem("stage2_made")
        prod_made = sem("prod_made")
        nodes_made = sem("nodes_made")
        xh_made = sem("xh_made")
        table0_stored = sem("table0_stored")
        table1_stored = sem("table1_stored")

        in_loaded = [sem(f"in_loaded{u}") for u in range(RING)]
        idx_loaded = [sem(f"idx_loaded{u}") for u in range(RING)]
        gathered = [[sem(f"gathered{u}{q}") for q in (0, 1)] for u in range(RING)]
        pairs_begun = sem("pairs_begun")
        slot_free = sem("slot_free")
        z_done = sem("z_done")
        hid_mm = sem("hid_mm")
        ef_mm = sem("ef_mm")
        pre_mm = sem("pre_mm")
        agg_mm = sem("agg_mm")
        tw_made = sem("tw_made")
        hid_made = sem("hid_made")
        ef_made = sem("ef_made")
        pre_made = sem("pre_made")
        msg_made = sem("msg_made")
        acc_added = sem("acc_added")
        hot_made = sem("hot_made")
        rel_made = sem("rel_made")
        rel1_made = sem("rel1_made")
        x1_chain = sem("x1_chain")
        x1_stats = sem("x1_stats")
        out_chain = sem("out_chain")

        counts_moved = sem("counts_moved")
        acc_staged = sem("acc_staged")
        upd_mm = sem("upd_mm")
        x1_made = sem("x1_made")
        normed1 = sem("normed1")
        staged1 = sem("staged1")
        turned1 = sem("turned1")
        acc1_made = sem("acc1_made")

        idx1_loaded = [sem(f"idx1_loaded{u}") for u in range(RING)]
        gathered1 = [[sem(f"gathered1{u}{q}") for q in (0, 1)] for u in range(RING)]
        slot1_free = sem("slot1_free")
        hot1_made = sem("hot1_made")
        acc1_added = sem("acc1_added")

        hid2_mm = sem("hid2_mm")
        hid2_made = sem("hid2_made")
        out_mm = sem("out_mm")
        out_made = sem("out_made")
        out_stored = sem("out_stored")

        N_PARAMS = 16
        block = ctx.enter_context(nc.Block())

        def group(ap, g):
            return ap[:, bass.ds(g * GT, GT)]

        def acc_group(g, which=0):
            v = acc[:, which, 0:N_PAD].rearrange("f (p t) -> f t p", t=NT)
            return v[:, bass.ds(g * GT, GT), :]

        @block.sync
        def _(sp):
            for g in range(NG):
                sp.dma_start(xs[:, g * GT:(g + 1) * GT, :],
                             x[:, g * GT * D:(g + 1) * GT * D].rearrange("p (t d) -> p t d", d=D))\
                  .then_inc(x_loaded[g], 16)
                if g == 0:
                    sp.dma_start(dst_b[:, :, :], dst_blocks).then_inc(dst_loaded, 16)
                    sp.dma_start(dst_t[:, :], dst_tiles).then_inc(dst_loaded, 16)
            for to, of in ((wn1a, Wn1[0:D, :]), (wn1b, Wn1[D:2 * D, :]), (we2, We2), (wn2, Wn2), (w1, W1), (w2, W2)):
                sp.dma_start(to[:, :], of).then_inc(params_loaded, 16)
            for q in (0, 1):
                sp.dma_start(we1[q * K_EDGE:(q + 1) * K_EDGE, :], We1).then_inc(params_loaded, 16)
            with nc.allow_non_contiguous_dma(reason="four bias columns"):
                for i, b in enumerate((be1, be2, bt, b1)):
                    sp.dma_start(cols[:, i:i + 1], b.rearrange("(p a) -> p a", a=1)).then_inc(params_loaded, 16)
            for to, b in ((bn1_r, bn1), (bn2_r, bn2), (b2_r, b2)):
                sp.dma_start(to[:, :], b.rearrange("(a d) -> a d", a=1).to_broadcast([P, D])).then_inc(params_loaded, 16)
            sp.dma_start(wt_f[:, :], Wt.to_broadcast([ZK, D])).then_inc(params_loaded, 16)
            sp.dma_start(ew_f[:, :], ew).then_inc(ew_loaded, 16)

            sp.wait_ge(base_made, 2)
            sp.dma_start(base_d.rearrange("(p j) -> p j", j=NBJ), least[:, :]).then_inc(base_stored, 16)
            sp.dma_start(span_d.rearrange("(p j) -> p j", j=NBJ), span[:, :]).then_inc(base_stored, 16)
            sp.wait_ge(base_stored, 32)
            one_row = base_d.rearrange("(a n) -> a n", a=1)
            sp.dma_start(base_first[:, :], one_row).then_inc(base_loaded, 16)
            sp.dma_start(span_row[:, :], span_d.rearrange("(a n) -> a n", a=1)).then_inc(base_loaded, 16)
            sp.dma_start(base_all[:, :], one_row.to_broadcast([P, NB])).then_inc(base_loaded, 16)

            sp.wait_ge(ew_split, 2)
            for k in range(NP3):
                for i in range(NP3):
                    sp.dma_start(ew_rows[NP3 * k + i, :].rearrange("(p c) -> p c", p=P), ew_p[:, i, :])\
                      .then_inc(ew_stored, 16)
                sp.dma_start(wt9[NP3 * k:NP3 * k + NP3, :], wt_p[NP3 * k:NP3 * k + NP3, k, :])\
                  .then_inc(wt_placed, 16)

            t0 = table0.rearrange("(p t) d -> p t d", t=NT)
            with sp.Fori(0, NG) as g:
                sp.wait_ge(nodes_made, g + 2)
                sp.dma_start(t0[:, bass.ds(g * GT, GT), :], nodes[:, bass.ds(g * GT, GT), :]).then_inc(table0_stored, 16)
            sp.wait_ge(ew_stored, 16 * ZK)

            sp.wait_ge(sweeps_made, 1)
            sweeps = sp.value_load(sweeps_s[0:1, 0:1], min_val=1, max_val=MAX_SWEEPS)
            ew_v = ew_rows.rearrange("k (n q c) -> k n q c", q=2, c=BLK)
            with sp.Fori(0, sweeps) as s:
                with sp.Fori(0, NBODY) as b:
                    for u in range(RING):
                        pair = b * RING + u
                        sp.wait_ge(slot_free, s * NPAIR + b * RING + u + 1)
                        sp.dma_start(idx[:, u, :], src[bass.ds(pair, 1), :, :].rearrange("a p t -> p (a t)"))\
                          .then_inc(idx_loaded[u], 16)
                        sp.dma_start(ea_s[:, u, :], ea[bass.ds(pair, 1), :, :].rearrange("a p c -> p (a c)"))\
                          .then_inc(in_loaded[u], 16)
                        sp.dma_start(ew_s[:, u, :, :], ew_v[:, bass.ds(pair, 1), :, :].rearrange("k a q c -> k (a q) c"))\
                          .then_inc(in_loaded[u], 16)

            sp.wait_ge(acc_added, sweeps * NB)
            sp.dma_start(count_n[:, :], acc[0:1, 1, 0:N_PAD].rearrange("a (p t) -> a p t", t=NT)).then_inc(counts_moved, 16)

            t1 = table1.rearrange("(p t) d -> p t d", t=NT)
            with sp.Fori(0, NG) as g:
                sp.wait_ge(normed1, g + 1)
                sp.dma_start(t1[:, bass.ds(g * GT, GT), :], nodes[:, bass.ds(g * GT, GT), :]).then_inc(table1_stored, 16)

            with sp.Fori(0, sweeps) as s:
                with sp.Fori(0, NBODY) as b:
                    for u in range(RING):
                        pair = b * RING + u
                        sp.wait_ge(slot1_free, s * NPAIR + b * RING + u + 1)
                        sp.dma_start(idx[:, u, :], src[bass.ds(pair, 1), :, :].rearrange("a p t -> p (a t)"))\
                          .then_inc(idx1_loaded[u], 16)

            ov = out.rearrange("p (t d) -> p t d", d=D)
            with sp.Fori(0, NG) as g:
                sp.wait_ge(out_made, g + 2)
                sp.dma_start(ov[:, bass.ds(g * GT, GT), :], xs[:, bass.ds(g * GT, GT), :]).then_inc(out_stored, 16)
            sp.wait_ge(out_stored, 16 * NG)

        @block.gpsimd
        def _(pool):
            pool.memset(ident[:, :], 0.0).then_inc(consts_made, 1)
            pool.memset(ones[:, :].bitcast(F32), 1.0).then_inc(consts_made, 1)
            pool.iota(iota_s[:, :], pattern=[[1, W]], base=0, channel_multiplier=0,
                      allow_small_or_imprecise_dtypes=True).then_inc(consts_made, 1)
            pool.wait_ge(consts_made, 3)
            pool.affine_select(out=ident[:, :], in_=ident[:, :], compare_op=ALU.not_equal, fill=1.0,
                               base=0, pattern=[[-1, P]], channel_multiplier=1).then_inc(consts_made, 1)
            pool.wait_ge(sweeps_made, 1)
            sweeps = pool.value_load(sweeps_s[0:1, 0:1], min_val=1, max_val=MAX_SWEEPS)

            def gathers(table, loaded, free, landed):
                with pool.Fori(0, sweeps * NBODY) as b:
                    for u in range(RING):
                        pool.wait_ge(free, b * RING + u + 1)
                        pool.wait_ge(loaded[u], b * 16 + 16)
                        pool.sem_inc(pairs_begun, 1)
                        for q in (0, 1):
                            for t in range(TB):
                                at = q * TB + t
                                pool.indirect_dma_start(
                                    rows[:, u, q, t, :], None, table,
                                    bass.IndirectOffsetOnAxis(ap=idx[:, u, at:at + 1], axis=0))\
                                    .then_inc(landed[u][q], 16)

            pool.wait_ge(table0_stored, 16 * NG)
            gathers(table0, idx_loaded, slot_free, gathered)
            pool.wait_ge(table1_stored, 16 * NG)
            gathers(table1, idx1_loaded, slot1_free, gathered1)

        @block.scalar
        def _(act):
            def root(which):
                act.wait_ge(var_made, which)
                act.activation(var[:, :], var[:, :], ACT.Sqrt).then_inc(root_made, 1)

            root(1)
            act.wait_ge(stats_made, 1)
            with act.Fori(0, NG) as g:
                for u in range(GT):
                    if u == 0:
                        act.wait_ge(turned, g + 1)
                        act.wait_ge(xh_made, g + 1)
                    t = g * GT + u
                    i = act.activation(stage[:, u, :], xs[:, bass.ds(t, 1), :].rearrange("p a d -> p (a d)"), ACT.Relu,
                                       bias=shift[:, bass.ds(t, 1)], scale=rstd[:, bass.ds(t, 1)])
                i.then_inc(normed, 1)

            act.wait_ge(sweeps_made, 1)
            sweeps = act.value_load(sweeps_s[0:1, 0:1], min_val=1, max_val=MAX_SWEEPS)

            def sigmoid(q, n):
                act.wait_ge(z_done, n)
                act.activation(tw[:, q, :], p_z, ACT.Sigmoid, bias=bt_c).then_inc(tw_made, 1)

            def hidden(q, n):
                act.wait_ge(hid_mm, n)
                act.activation(hid[:, q, :], p_hid[q], ACT.Relu, bias=be1_c).then_inc(hid_made, 1)

            def message(q, n):
                act.wait_ge(pre_made, n)
                m = msg[:, q, :, :].rearrange("p t d -> p (t d)")
                act.activation(m, m, ACT.Relu).then_inc(msg_made, 1)

            def pair_step(b, u, first):
                n = b * (2 * RING) + 2 * u
                if not first:
                    act.wait_ge(ef_made, n)
                sigmoid(0, n + 1)
                hidden(0, n + 1)
                if not first:
                    message(0, n - 1)
                hidden(1, n + 2)
                sigmoid(1, n + 2)
                if not first:
                    message(1, n)

            act.wait_ge(params_loaded, 16 * N_PARAMS)
            for u in range(RING):
                pair_step(0, u, u == 0)
            with act.Fori(1, sweeps * NBODY) as b:
                for u in range(RING):
                    pair_step(b, u, False)
            message(0, sweeps * NB)
            message(1, sweeps * NB)

            act.wait_ge(acc_added, sweeps * NB)
            with act.Fori(0, NG) as g:
                act.wait_ge(upd_mm, g + 1)
                act.activation(stage[:, :, :], acc_group(g), ACT.Copy).then_inc(acc_staged, 1)

            root(2)
            act.wait_ge(stats_made, 2)
            with act.Fori(0, NG) as g:
                for u in range(GT):
                    t = g * GT + u
                    i = act.activation(nodes[:, bass.ds(t, 1), :].rearrange("p a d -> p (a d)"),
                                       xs[:, bass.ds(t, 1), :].rearrange("p a d -> p (a d)"), ACT.Relu,
                                       bias=shift[:, bass.ds(t, 1)], scale=rstd[:, bass.ds(t, 1)])
                i.then_inc(normed1, 1)

            with act.Fori(0, NG) as g:
                act.wait_ge(hid2_mm, g + 1)
                act.wait_ge(out_mm, g + 1)
                act.activation(stage[:, :, :], p_turn, ACT.Relu, bias=b1_c).then_inc(hid2_made, 1)

        @block.tensor
        def _(pe):
            pe.wait_ge(consts_made, 4)
            pe.wait_ge(params_loaded, 16 * N_PARAMS)
            pe.sem_inc(turned, 1)
            with pe.Fori(0, NG) as g:
                pe.wait_ge(normed, g + 1)
                pe.wait_ge(stage2_made, g + 1)
                for u in range(GT):
                    i = pe.transpose(p_turn[:, u, :], stage[:, u, :], ident[:, :])
                i.then_inc(turned, 1)
                pe.wait_ge(stage2_made, g + 2)
                pe.wait_ge(nodes_made, g + 1)
                for u in range(GT):
                    i = pe.matmul(p_prod[:, u, :], stage2[:, u, :], wn1a[:, :], start=True, stop=True)
                i.then_inc(prod_made, 1)

            pe.wait_ge(sweeps_made, 1)
            sweeps = pe.value_load(sweeps_s[0:1, 0:1], min_val=1, max_val=MAX_SWEEPS)
            hot_f = hot[:, :, :, :].bitcast(F32)

            def weight_product(u, q):
                pe.matmul(p_z, wt9[:, :], ew_s[:, u, q, :], start=True, stop=True).then_inc(z_done, 1)

            def hidden_product(u, q):
                k = slice(q * K_EDGE, (q + 1) * K_EDGE)
                pe.matmul(p_hid[q], we1[k, :], ea_s[k, u, :], start=True, stop=True).then_inc(hid_mm, 1)

            def edge_product(q, n):
                pe.wait_ge(hid_made, n)
                pe.matmul(p_ef[q], we2[:, :], hid[:, q, :], start=True, stop=True).then_inc(ef_mm, 1)

            def message_product(q, n):
                pe.wait_ge(ef_made, n)
                for t in range(TB):
                    i = pe.matmul(p_pre[q][:, t * D:(t + 1) * D], ef[:, q, t * P:(t + 1) * P], wn1b[:, :],
                                  start=True, stop=True)
                i.then_inc(pre_mm, 1)

            def aggregate(n):
                pe.wait_ge(msg_made, n)
                pe.wait_ge(hot_made, n)
                for q in (0, 1):
                    for t in range(TB):
                        pe.matmul(p_agg[:, q, 0, :], msg[:, q, t, :], hot_f[:, q, t, :],
                                  start=(t == 0), stop=(t == TB - 1))
                    for t in range(TB):
                        i = pe.matmul(p_agg[:, q, 1, :], ones[:, :], hot[:, q, t, :],
                                      start=(t == 0), stop=(t == TB - 1))
                i.then_inc(agg_mm, 1)

            def pair_step(b, u, first):
                n = b * (2 * RING) + 2 * u
                pe.wait_ge(in_loaded[u], b * 32 + 32)
                weight_product(u, 0)
                hidden_product(u, 0)
                hidden_product(u, 1)
                edge_product(0, n + 1)
                pe.wait_ge(tw_made, n + 1)
                weight_product(u, 1)
                edge_product(1, n + 2)
                if not first:
                    aggregate(n)
                message_product(0, n + 1)
                message_product(1, n + 2)

            pe.wait_ge(wt_placed, 16 * NP3)
            pe.wait_ge(nodes_made, NG + 1)
            for u in range(RING):
                pair_step(0, u, u == 0)
            with pe.Fori(1, sweeps * NBODY) as b:
                for u in range(RING):
                    pair_step(b, u, False)
            aggregate(sweeps * NB)

            pe.sem_inc(upd_mm, 1)
            with pe.Fori(0, NG) as g:
                pe.wait_ge(acc_staged, g + 1)
                pe.wait_ge(x1_made, g + 1)
                for u in range(GT):
                    i = pe.matmul(p_prod[:, u, :], stage[:, u, :], wn2[:, :], start=True, stop=True)
                i.then_inc(upd_mm, 1)

            with pe.Fori(0, NG) as g:
                pe.wait_ge(staged1, g + 1)
                pe.wait_ge(acc1_made, g + 1)
                for u in range(GT):
                    i = pe.transpose(p_turn[:, u, :], stage2[:, u, :], ident[:, :])
                i.then_inc(turned1, 1)

            pe.sem_inc(slot1_free, RING)
            with pe.Fori(0, sweeps * NBODY) as b:
                for u in range(RING):
                    n = b * (2 * RING) + 2 * u
                    pe.wait_ge(hot1_made, n + 2)
                    for q in (0, 1):
                        pe.wait_ge(gathered1[u][q], b * (16 * TB) + 16 * TB)
                        for t in range(TB):
                            i = pe.matmul(p_agg[:, q, 0, :], rows[:, u, q, t, :], hot_f[:, q, t, :],
                                          start=(t == 0), stop=(t == TB - 1))
                    i.then_inc(slot1_free, 1)

            pe.wait_ge(acc1_added, sweeps * NB)
            pe.sem_inc(out_mm, 1)
            with pe.Fori(0, NG) as g:
                h = acc_group(g)
                pe.wait_ge(hid2_made, g + 1)
                pe.matmul(p_turn[:, 0:4, :], w1[:, :], h[:, 0:4, :], start=True, stop=True)
                pe.matmul(p_turn[:, 4:GT, :], w1[:, :], h[:, 4:GT, :], start=True, stop=True).then_inc(hid2_mm, 1)
                pe.wait_ge(hid2_made, g + 2)
                pe.wait_ge(out_made, g + 1)
                for u in range(GT):
                    i = pe.matmul(p_prod[:, u, :], stage[:, u, :], w2[:, :], start=True, stop=True)
                i.then_inc(out_mm, 1)

        @block.vector
        def _(dve):
            step = [0]

            def chain(instruction):
                step[0] += 1
                return instruction.then_inc(dve_chain, 1)

            def settle():
                dve.wait_ge(dve_chain, step[0])

            chain(dve.memset(acc[:, :, :], 0.0))
            chain(dve.memset(stats[:, :, :], 0.0))

            dve.wait_ge(dst_loaded, 32)
            chain(dve.tensor_reduce(least[:, :], dst_b[:, :, :], AX.X, ALU.min))
            chain(dve.tensor_reduce(span[:, :], dst_b[:, :, :], AX.X, ALU.max))
            settle()
            dve.tensor_tensor(span[:, :], span[:, :], least[:, :], ALU.subtract).then_inc(base_made, 2)

            dve.wait_ge(ew_loaded, 16)
            dve.wait_ge(params_loaded, 16 * N_PARAMS)
            for whole, parts in ((ew_f, ew_p), (wt_f, wt_p)):
                for i in range(NP3):
                    last = dve.tensor_copy(parts[:, i, :], whole[:, :])
                    if i < NP3 - 1:
                        chain(last)
                        settle()
                        chain(dve.tensor_tensor(whole[:, :], whole[:, :], parts[:, i, :], ALU.subtract))
                        settle()
                last.then_inc(ew_split, 1)

            def layer_norm_scales(which):
                m_even, s_even, m_odd, s_odd = (stats[:, :, i] for i in (1, 2, 4, 5))
                chain(dve.tensor_tensor(mean[:, :], m_even, m_odd, ALU.add))
                chain(dve.tensor_tensor(half[:, :], m_even, m_odd, ALU.subtract))
                chain(dve.tensor_tensor(var[:, :], s_even, s_odd, ALU.add))
                settle()
                chain(dve.tensor_scalar(mean[:, :], mean[:, :], 0.5, None, ALU.mult))
                chain(dve.tensor_scalar(half[:, :], half[:, :], 0.5, None, ALU.mult))
                settle()
                chain(dve.tensor_tensor(half[:, :], half[:, :], half[:, :], ALU.mult))
                settle()
                chain(dve.scalar_tensor_tensor(out=var[:, :], in0=var[:, :], scalar=1.0 / D, in1=half[:, :],
                                               op0=ALU.mult, op1=ALU.add))
                settle()
                dve.tensor_scalar(var[:, :], var[:, :], EPS, None, ALU.add).then_inc(var_made, 1)
                dve.wait_ge(root_made, which)
                chain(dve.reciprocal(rstd[:, :], var[:, :]))
                settle()
                dve.scalar_tensor_tensor(out=shift[:, :], in0=mean[:, :], scalar=-1.0, in1=rstd[:, :],
                                         op0=ALU.mult, op1=ALU.mult).then_inc(stats_made, 1)

            for g in range(NG):
                dve.wait_ge(x_loaded[g], 16)
                for t in range(g * GT, (g + 1) * GT):
                    i = dve.bn_stats(stats[:, t, :], xs[:, t, :])
            chain(i)
            settle()
            layer_norm_scales(1)

            dve.sem_inc(stage2_made, 1)
            dve.sem_inc(nodes_made, 1)
            dve.sem_inc(xh_made, 1)
            dve.wait_ge(params_loaded, 16 * N_PARAMS)
            bn1_g = bn1_r[:, :].rearrange("p (a d) -> p a d", a=1).to_broadcast([P, GT, D])
            with dve.Fori(0, NG) as g:
                dve.wait_ge(normed, g + 1)
                dve.tensor_tensor(group(xs, g), group(xs, g), stage[:, :, :], ALU.add).then_inc(xh_made, 1)
                dve.wait_ge(turned, g + 2)
                dve.tensor_copy(stage2[:, :, :], p_turn).then_inc(stage2_made, 1)
                dve.wait_ge(prod_made, g + 1)
                dve.tensor_tensor(group(nodes, g), p_prod, bn1_g, ALU.add).then_inc(nodes_made, 1)

            dve.wait_ge(base_loaded, 48)
            chain(dve.tensor_reduce(sweeps_s[:, :], span_row[:, :], AX.X, ALU.max))
            settle()
            chain(dve.tensor_scalar(sweeps_s[:, :], sweeps_s[:, :], W_LOG2, None, ALU.logical_shift_right))
            settle()
            dve.tensor_scalar(sweeps_s[:, :], sweeps_s[:, :], 1, None, ALU.add).then_inc(sweeps_made, 1)
            dve.wait_ge(sweeps_made, 1)
            sweeps = dve.value_load(sweeps_s[0:1, 0:1], min_val=1, max_val=MAX_SWEEPS)

            chain(dve.tensor_copy(p_iota, iota_s[:, :]))

            def first_windows():
                chain(dve.tensor_copy(base_now[:, :], base_first[:, :]))
                chain(dve.tensor_tensor(rel[:, :].rearrange("p (n t) -> p n t", t=TB),
                                        dst_t[:, :].rearrange("p (n t) -> p n t", t=TB),
                                        base_all[:, :].rearrange("p (n a) -> p n a", a=1).to_broadcast([P, NB, TB]),
                                        ALU.subtract))
                settle()
                chain(dve.memset(rel[:, FULL_TILES + (TAIL > 0):NTILE], -float(2 * N_PAD)))
                if TAIL:
                    chain(dve.memset(rel[TAIL:P, FULL_TILES:FULL_TILES + 1], -float(2 * N_PAD)))
                settle()

            def next_windows(done, n):
                dve.tensor_scalar(rel[:, :], rel[:, :], float(W), None, ALU.subtract).then_inc(done, 1)
                dve.tensor_scalar(base_now[:, :], base_now[:, :], W, N_PAD, ALU.add, ALU.min).then_inc(done, 1)
                dve.wait_ge(done, n * 2 + 2)

            iota_t = p_iota.rearrange("p (a w) -> p a w", a=1).to_broadcast([P, TB, W])

            def one_hot(b, u, q):
                at = b * (RING * 2 * TB) + (2 * u + q) * TB
                r = rel[:, bass.ds(at, TB)].rearrange("p (t a) -> p t a", a=1).to_broadcast([P, TB, W])
                return dve.tensor_tensor(hot[:, q, :, :], iota_t, r, ALU.is_equal)

            first_windows()
            dve.sem_inc(slot_free, RING)

            def window_base(blk):
                return dve.value_load(base_now[0:1, bass.ds(blk, 1)], min_val=0, max_val=N_PAD)

            def add_sums(total, blk, pairs):
                starts = [window_base(blk + q) for q in (0, 1)]
                dve.wait_ge(agg_mm, pairs)
                for q, at in enumerate(starts):
                    to = acc[:, :, bass.ds(at, W)]
                    dve.wait_ge(acc_added, total + q)
                    dve.tensor_tensor(to, p_agg[:, q, :, :], to, ALU.add).then_inc(acc_added, 1)

            def pair_step(s, b, u, first):
                total = s * NB + b * (2 * RING) + 2 * u
                for q in (0, 1):
                    dve.wait_ge(ef_mm, total + q + 1)
                    dve.wait_ge(tw_made, total + q + 1)
                    dve.scalar_tensor_tensor(out=ef[:, q, :], in0=p_ef[q], scalar=be2_c, in1=tw[:, q, :],
                                             op0=ALU.add, op1=ALU.mult).then_inc(ef_made, 1)
                if not first:
                    add_sums(total - 2, b * (2 * RING) + 2 * u - 2, s * NPAIR + b * RING + u)
                for q in (0, 1):
                    one_hot(b, u, q).then_inc(hot_made, 1)
                for q in (0, 1):
                    dve.wait_ge(pre_mm, total + q + 1)
                    dve.wait_ge(gathered[u][q], (s * NBODY + b) * (16 * TB) + 16 * TB)
                    dve.tensor_tensor(msg[:, q, :, :].rearrange("p t d -> p (t d)"), p_pre[q],
                                      rows[:, u, q, :, :].rearrange("p t d -> p (t d)"), ALU.add)\
                       .then_inc(pre_made, 1)
                dve.wait_ge(pre_made, total + 2)
                dve.sem_inc(slot_free, 1)

            with dve.Fori(0, sweeps) as s:
                for u in range(RING):
                    pair_step(s, 0, u, u == 0)
                with dve.Fori(1, NBODY) as b:
                    for u in range(RING):
                        pair_step(s, b, u, False)
                add_sums(s * NB + NB - 2, NB - 2, s * NPAIR + NPAIR)
                dve.wait_ge(acc_added, s * NB + NB)
                next_windows(rel_made, s)

            dve.sem_inc(x1_made, 1)
            dve.wait_ge(counts_moved, 16)
            bn2_g = bn2_r[:, :].rearrange("p (a d) -> p a d", a=1).to_broadcast([P, GT, D])
            with dve.Fori(0, NG) as g:
                c = count_n[:, bass.ds(g * GT, GT)].rearrange("p (t a) -> p t a", a=1).to_broadcast([P, GT, D])
                dve.tensor_tensor(stage2[:, :, :], bn2_g, c, ALU.mult).then_inc(x1_chain, 1)
                dve.wait_ge(x1_chain, g * 2 + 1)
                dve.tensor_tensor(group(xs, g), group(xs, g), stage2[:, :, :], ALU.add).then_inc(x1_chain, 1)
                dve.wait_ge(upd_mm, g + 2)
                dve.wait_ge(x1_chain, g * 2 + 2)
                dve.tensor_tensor(group(xs, g), group(xs, g), p_prod, ALU.add).then_inc(x1_made, 1)
                dve.wait_ge(x1_made, g + 2)
                for u in range(GT):
                    t = g * GT + u
                    i = dve.bn_stats(stats[:, bass.ds(t, 1), :].rearrange("p a s -> p (a s)"),
                                     xs[:, bass.ds(t, 1), :].rearrange("p a d -> p (a d)"))
                i.then_inc(x1_stats, 1)
            dve.wait_ge(x1_stats, NG)
            layer_norm_scales(2)

            dve.sem_inc(acc1_made, 1)
            with dve.Fori(0, NG) as g:
                dve.wait_ge(normed1, g + 1)
                dve.tensor_copy(stage2[:, :, :], group(nodes, g)).then_inc(staged1, 1)
                dve.wait_ge(turned1, g + 1)
                dve.tensor_copy(acc_group(g), p_turn).then_inc(acc1_made, 1)
            first_windows()
            dve.wait_ge(acc1_made, NG + 1)

            def add_sums1(total, blk, pairs):
                starts = [window_base(blk + q) for q in (0, 1)]
                dve.wait_ge(slot1_free, pairs + RING)
                for q, at in enumerate(starts):
                    to = acc[:, 0, bass.ds(at, W)]
                    dve.wait_ge(acc1_added, total + q)
                    dve.tensor_tensor(to, p_agg[:, q, 0, :], to, ALU.add).then_inc(acc1_added, 1)

            def pair_step1(s, b, u):
                total = s * NB + b * (2 * RING) + 2 * u
                for q in (0, 1):
                    one_hot(b, u, q).then_inc(hot1_made, 1)
                add_sums1(total, b * (2 * RING) + 2 * u, s * NPAIR + b * RING + u + 1)

            with dve.Fori(0, sweeps) as s:
                with dve.Fori(0, NBODY) as b:
                    for u in range(RING):
                        pair_step1(s, b, u)
                dve.wait_ge(acc1_added, s * NB + NB)
                next_windows(rel1_made, s)

            dve.sem_inc(hid2_made, 1)
            dve.sem_inc(out_made, 1)
            b2_g = b2_r[:, :].rearrange("p (a d) -> p a d", a=1).to_broadcast([P, GT, D])
            with dve.Fori(0, NG) as g:
                dve.wait_ge(out_mm, g + 2)
                dve.tensor_tensor(stage2[:, :, :], p_prod, b2_g, ALU.add).then_inc(out_chain, 1)
                dve.wait_ge(out_chain, g + 1)
                dve.scalar_tensor_tensor(out=group(xs, g), in0=stage2[:, :, :], scalar=0.0, in1=group(xs, g),
                                         op0=ALU.max, op1=ALU.add).then_inc(out_made, 1)


def kernel(x, src, dst, edge_attr_64, edge_weight, **w):
    import numpy as np
    import concourse.bacc as bacc
    from concourse.bass_utils import run_bass_kernel_spmd

    x, src, dst, ea, ew = (np.asarray(a) for a in (x, src, dst, edge_attr_64, edge_weight))
    extra = E_PAD - N_EDGES
    src = np.pad(src, (0, extra))
    dst = np.pad(dst, (0, extra), mode="edge")
    ea = np.pad(ea, ((0, extra), (0, 0)))
    arrays = {
        "x": np.pad(x, ((0, N_PAD - N_NODES), (0, 0))).reshape(P, NT * D),
        "ea": ea.reshape(NPAIR, 2, BLK, K_EDGE).transpose(0, 1, 3, 2).reshape(NPAIR, P, BLK),
        "ew": np.pad(ew, (0, extra)).reshape(P, E_PAD // P),
        "src": src.reshape(NPAIR, 2 * TB, P).transpose(0, 2, 1),
        "dst_tiles": dst.reshape(NTILE, P).T,
        "dst_blocks": dst.reshape(NBP, NBJ, BLK),
    }
    names = {"We1": "L0_gnn_We1", "be1": "L0_gnn_be1", "We2": "L0_gnn_We2", "be2": "L0_gnn_be2", "Wt": "L0_gnn_Wt",
             "bt": "L0_gnn_bt", "Wn1": "L0_gnn_Wn1", "bn1": "L0_gnn_bn1", "Wn2": "L0_gnn_Wn2", "bn2": "L0_gnn_bn2",
             "W1": "L1_gnn_W1", "b1": "L1_gnn_b1", "W2": "L1_gnn_W2", "b2": "L1_gnn_b2"}
    for short, name in names.items():
        arrays[short] = np.asarray(w[name])
    arrays = {k: np.ascontiguousarray(a) for k, a in arrays.items()}
    nc = bacc.Bacc("TRN2", target_bir_lowering=False, num_devices=1)
    args = {k: nc.dram_tensor(f"in_{k}", a.shape, mybir.dt.from_np(a.dtype), kind="ExternalInput").ap()
            for k, a in arrays.items()}
    out = nc.dram_tensor("out", (P, NT * D), F32, kind="ExternalOutput").ap()
    gnn_program(nc, **args, out=out)
    r = run_bass_kernel_spmd(nc, [{f"in_{k}": a for k, a in arrays.items()}], core_ids=[0])
    return r.results[0]["out"].reshape(N_PAD, D)[:N_NODES]
```

```python
from contextlib import ExitStack

import concourse.bass as bass
from concourse import mybir

F32 = mybir.dt.float32
F32R = mybir.dt.float32r
BF16 = mybir.dt.bfloat16
F16 = mybir.dt.float16
I32 = mybir.dt.int32
ALU = mybir.AluOpType
ACT = mybir.ActivationFunctionType
AX = mybir.AxisListType

P = 128
D = 128
K_EDGE = 64
N_NODES = 6250
N_EDGES = 200000
EPS = 1e-5

NT = -(-N_NODES // P)
GT = 7
NG = NT // GT
N_PAD = NT * P
assert NG * GT == NT

TB = 4
BLK = TB * P
RING = 4
NPAIR = -(-N_EDGES // (2 * BLK * RING)) * RING
NBODY = NPAIR // RING
NB = 2 * NPAIR
NTILE = NB * TB
E_PAD = NTILE * P

W_LOG2 = 6
W = 1 << W_LOG2
ACC = N_PAD + W
NBP = 98
NBJ = NB // NBP
assert NBP * NBJ == NB
MAX_SWEEPS = N_PAD // W + 1
FULL_TILES = N_EDGES // P
TAIL = N_EDGES % P
assert TAIL in (0, 32, 64, 96)

CW = 10
CK = CW * NT
VT = 6
VH = VT // 2
CB = 4
NCB = 28
NWIN = CB * NCB
C_NODES = NWIN * CW
assert CK <= 512 and NWIN <= P and NCB < NBODY
ROUND = 1.5 * 2.0 ** 23
VISIT = 2048
MAX_VISITS = -(-NTILE // VT)
assert NTILE <= VISIT and VISIT * (MAX_VISITS + 1) < 2 ** 24

NP3 = 3
ZK = NP3 * NP3


def gnn_program(nc, x, ea, ew, src, src_tiles, dst_tiles, dst_blocks, We1, be1, We2, be2, Wt, bt, Wn1, bn1, Wn2, bn2,
                W1, b1, W2, b2, out):
    ctx = ExitStack()
    with ctx:
        def sb(name, shape, dt=F32):
            return ctx.enter_context(nc.sbuf_tensor(name, shape, dt))

        def sem(name):
            return ctx.enter_context(nc.semaphore(name))

        def dram(name, shape, dt=F32):
            return nc.dram_tensor(name, shape, dt, kind="Internal").ap()

        table0 = dram("table0", (N_PAD, D))
        table1 = dram("table1", (N_PAD, NP3 * D), BF16)
        ew_rows = dram("ew_rows", (ZK, E_PAD), BF16)
        base_d = dram("base_d", (NB,), I32)
        great_d = dram("great_d", (NB,), I32)
        tleast_d = dram("tleast_d", (NTILE,), I32)
        tgreat_d = dram("tgreat_d", (NTILE,), I32)
        win_d = dram("win_d", (NWIN,), I32)

        xs = sb("xs", [P, NT, D])
        nodes = sb("nodes", [P, NT, D])
        acc = sb("acc", [P, 2, ACC])
        stats = sb("stats", [P, NT, 6])
        mean = sb("mean", [P, NT])
        half = sb("half", [P, NT])
        var = sb("var", [P, NT])
        rstd = sb("rstd", [P, NT])
        shift = sb("shift", [P, NT])
        count_n = sb("count_n", [P, NT])

        we1 = sb("we1", [P, D])
        we2 = sb("we2", [P, D])
        wn1a = sb("wn1a", [P, D])
        wn1b = sb("wn1b", [P, D])
        wn2 = sb("wn2", [P, D])
        w1 = sb("w1", [P, D])
        w2 = sb("w2", [P, D])
        cols = sb("cols", [P, 4])
        be1_c, be2_c, bt_c, b1_c = (cols[:, i:i + 1] for i in range(4))
        bn1_r = sb("bn1_r", [P, D])
        bn2_r = sb("bn2_r", [P, D])
        b2_r = sb("b2_r", [P, D])
        wt_f = sb("wt_f", [ZK, D])
        wt_p = sb("wt_p", [ZK, NP3, D], BF16)
        wt9 = sb("wt9", [ZK, D], BF16)
        ones = sb("ones", [P, P], F32R)
        iota_s = sb("iota_s", [P, W])

        EC = E_PAD // P
        CROW = CB * CW
        HOT = VT * (P + CK) // 2
        sizes = [EC, NP3 * EC // 2, RING * BLK, RING * BLK, 2 * BLK]
        arena = sb("arena", [P, max(sum(sizes), 2 * (NTILE + VT) + 2 * NT * CROW + HOT)])
        cuts = [sum(sizes[:i]) for i in range(len(sizes) + 1)]
        ew_f, ew_p, ea_s, ew_s, hid = (arena[:, a:b] for a, b in zip(cuts, cuts[1:]))
        ew_p = ew_p.bitcast(BF16).rearrange("p (i c) -> p i c", i=NP3)
        ea_s = ea_s.rearrange("p (u c) -> p u c", u=RING)
        ew_s = ew_s[0:ZK, :].bitcast(BF16).rearrange("p (u q c) -> p u q c", u=RING, q=2)
        hid = hid.rearrange("p (q c) -> p q c", q=2)
        src_b_all, key_all = (arena[:, i * (NTILE + VT):(i + 1) * (NTILE + VT)] for i in range(2))
        src_b, key = src_b_all[:, 0:NTILE], key_all[:, 0:NTILE]
        at = 2 * (NTILE + VT)
        src_t, rel_add = (arena[:, at + i * NTILE:at + (i + 1) * NTILE] for i in range(2))
        src_i = rel_add.bitcast(I32)
        c_sums = [arena[:, at + j * NT * CROW:at + (j + 1) * NT * CROW].rearrange("p (a n) -> p a n", a=NT) for j in (0, 1)]
        at += 2 * NT * CROW
        hot_src = arena[:, at:at + VT * P // 2].bitcast(BF16).rearrange("p (t c) -> p t c", t=VT)
        at += VT * P // 2
        hot_key = arena[:, at:at + VT * CK // 2].bitcast(BF16).rearrange("p (t c) -> p t c", t=VT)
        c_rows = sb("c_rows", [CROW, D])
        dst_t = sb("dst_t", [P, NTILE], I32)
        least = sb("least", [NBP, NBJ], I32)
        great = sb("great", [NBP, NBJ], I32)
        base_all = sb("base_all", [P, NB], I32)
        base_now = sb("base_now", [1, NB], I32)
        great_all = sb("great_all", [P, NB], I32)
        params = sb("params", [1, 4], I32)
        blk_up = sb("blk_up", [1, NB])
        tleast = sb("tleast", [NBP, NBJ, TB], I32)
        tgreat = sb("tgreat", [NBP, NBJ, TB], I32)
        win_low = sb("win_low", [P, 1])
        win_n = sb("win_n", [P, 5])
        win_i = sb("win_i", [P, 1], I32)
        win_row = sb("win_row", [1, NWIN], I32)
        win_off = sb("win_off", [P, NWIN])
        iota_b = sb("iota_b", [P, P], F16)
        iota_k = sb("iota_k", [P, CK], F16)
        zeros = sb("zeros", [1, CK], BF16)
        rel = sb("rel", [P, NTILE])
        idx = sb("idx", [P, RING, 2 * TB], I32)
        RROW = RING * 2 * TB * D
        big = sb("big", [P, RROW * NP3 // 2])
        assert RROW * NP3 // 2 == RROW + 2 * TB * D + 2 * BLK
        rows = big[:, 0:RROW].rearrange("p (u q t d) -> p u q t d", u=RING, q=2, t=TB)
        msg_flat = big[:, RROW:RROW + 2 * TB * D]
        msg = msg_flat.rearrange("p (q t d) -> p q t d", q=2, t=TB)
        tw = big[:, RROW + 2 * TB * D:RROW + 2 * TB * D + 2 * BLK].rearrange("p (q c) -> p q c", q=2)
        rows1 = big[:, :].bitcast(BF16).rearrange("p (u q t i d) -> p u q t i d", u=RING, q=2, t=TB, i=NP3)
        parts = big[:, 0:2 * GT * D * NP3 // 2].bitcast(BF16).rearrange("p (s t i d) -> p s t i d", s=2, t=GT, i=NP3)
        left = big[:, GT * D * NP3:GT * D * NP3 + GT * D].rearrange("p (t d) -> p t d", t=GT)
        ef = sb("ef", [P, 2, BLK])
        stage, stage2 = (a.rearrange("p q c -> p (q c)")[:, 0:GT * D].rearrange("p (t d) -> p t d", t=GT)
                         for a in (tw, ef[:, :, :]))
        dst_b = big[0:NBP, 0:NBJ * BLK].bitcast(I32).rearrange("p (j c) -> p j c", j=NBJ)
        cand_row, span_row = msg_flat[0:1, 0:NB], msg_flat[0:1, NB:2 * NB].bitcast(I32)
        nodes_flat = nodes[:, :, :].rearrange("p t d -> p (t d)")
        tleast_all, tgreat_all = (nodes_flat[:, i * NTILE:(i + 1) * NTILE].bitcast(I32) for i in (0, 1))
        meets, tile_up = (nodes_flat[:, i * NTILE:(i + 1) * NTILE] for i in (2, 3))
        firsts = nodes_flat[:, 0:NTILE]
        assert 4 * NTILE <= NT * D
        hot = sb("hot", [P, 2, TB, W], F32R)

        hot1 = sb("hot1", [P, 2, TB, W], BF16)

        BANK = 512
        ps = ctx.enter_context(nc.psum_tensor("ps", [P, 8 * BANK], F32))
        p_hid = [ps[:, q * BANK:(q + 1) * BANK] for q in (0, 1)]
        p_z = ps[:, 2 * BANK:3 * BANK]
        p_ef = [ps[:, q * BANK:(q + 1) * BANK] for q in (3, 4)]
        p_pre = [ps[:, q * BANK:(q + 1) * BANK] for q in (5, 6)]
        p_agg = ps[:, 7 * BANK:7 * BANK + 4 * W].rearrange("p (q s w) -> p q s w", q=2, s=2)
        p_iota = ps[:, 7 * BANK + 4 * W:7 * BANK + 5 * W]
        p_c = [ps[:, q * BANK:q * BANK + CK] for q in (0, 1)]
        p_cs = ps[0:CROW, 2 * BANK:2 * BANK + D]
        p_cst = ps[:, 3 * BANK:3 * BANK + CROW]
        p_turn = ps[:, 0:GT * D].rearrange("p (t d) -> p t d", t=GT)
        p_prod = ps[:, 2 * BANK:2 * BANK + GT * D].rearrange("p (t d) -> p t d", t=GT)

        ident = sb("ident", [P, P])

        x_loaded = [sem(f"x_loaded{g}") for g in range(NG)]
        params_loaded = sem("params_loaded")
        dst_loaded = sem("dst_loaded")
        ew_loaded = sem("ew_loaded")
        consts_made = sem("consts_made")
        base_made = sem("base_made")
        base_stored = sem("base_stored")
        base_loaded = sem("base_loaded")
        sweeps_made = sem("sweeps_made")
        ew_split = sem("ew_split")
        ew_stored = sem("ew_stored")
        wt_placed = sem("wt_placed")
        dve_chain = sem("dve_chain")
        var_made = sem("var_made")
        root_made = sem("root_made")
        stats_made = sem("stats_made")
        normed = sem("normed")
        turned = sem("turned")
        stage2_made = sem("stage2_made")
        prod_made = sem("prod_made")
        nodes_made = sem("nodes_made")
        xh_made = sem("xh_made")
        table0_stored = sem("table0_stored")
        table1_stored = [sem(f"table1_stored{s}") for s in (0, 1)]

        in_loaded = [sem(f"in_loaded{u}") for u in range(RING)]
        idx_loaded = [sem(f"idx_loaded{u}") for u in range(RING)]
        gathered = [[sem(f"gathered{u}{q}") for q in (0, 1)] for u in range(RING)]
        pairs_begun = sem("pairs_begun")
        slot_free = sem("slot_free")
        z_done = sem("z_done")
        hid_mm = sem("hid_mm")
        ef_mm = sem("ef_mm")
        pre_mm = sem("pre_mm")
        agg_mm = sem("agg_mm")
        tw_made = sem("tw_made")
        hid_made = sem("hid_made")
        ef_made = sem("ef_made")
        pre_made = sem("pre_made")
        msg_made = sem("msg_made")
        acc_added = sem("acc_added")
        hot_made = sem("hot_made")
        rel_made = sem("rel_made")
        rel1_made = sem("rel1_made")
        windows_moved = sem("windows_moved")
        x1_chain = sem("x1_chain")
        x1_stats = sem("x1_stats")
        out_chain = sem("out_chain")

        counts_moved = sem("counts_moved")
        acc_staged = sem("acc_staged")
        upd_mm = sem("upd_mm")
        x1_made = sem("x1_made")
        normed1 = sem("normed1")
        staged1 = sem("staged1")
        turned1 = sem("turned1")
        acc1_made = sem("acc1_made")

        idx1_loaded = [sem(f"idx1_loaded{u}") for u in range(RING)]
        gathered1 = [[sem(f"gathered1{u}{q}") for q in (0, 1)] for u in range(RING)]
        slot1_free = sem("slot1_free")
        hot1_made = sem("hot1_made")
        acc1_added = sem("acc1_added")

        tile_ends_loaded = sem("tile_ends_loaded")
        tile_up_made = sem("tile_up_made")
        win_made = sem("win_made")
        win_stored = sem("win_stored")
        win_loaded = sem("win_loaded")
        src_loaded = sem("src_loaded")
        c_hot = sem("c_hot")
        c_hot_free = sem("c_hot_free")
        turns_begun = sem("turns_begun")
        c_built = sem("c_built")
        c_moved = sem("c_moved")
        c_done = sem("c_done")
        c_staged = sem("c_staged")
        c_turned = sem("c_turned")
        parts_first = sem("parts_first")
        parts_chain = sem("parts_chain")
        parts_made = sem("parts_made")
        c_added = sem("c_added")

        hid2_mm = sem("hid2_mm")
        hid2_made = sem("hid2_made")
        out_mm = sem("out_mm")
        out_made = sem("out_made")
        out_stored = sem("out_stored")

        N_PARAMS = 16
        block = ctx.enter_context(nc.Block())

        def load_params(engine):
            return (engine.value_load(params[0:1, 0:1], min_val=1, max_val=MAX_SWEEPS),
                    engine.value_load(params[0:1, 1:2], min_val=0, max_val=NBODY - NCB - 1),
                    engine.value_load(params[0:1, 2:3], min_val=NCB + 1, max_val=MAX_SWEEPS * NBODY),
                    engine.value_load(params[0:1, 3:4], min_val=NCB + 1, max_val=NBODY))

        def body_at(start, b):
            return nc.s_assert_within(start + b, 0, NBODY - 1,
                                      skip_runtime_bounds_check_because="b ends at NBODY - start")

        def group(ap, g):
            return ap[:, bass.ds(g * GT, GT)]

        def acc_group(g, which=0):
            v = acc[:, which, 0:N_PAD].rearrange("f (p t) -> f t p", t=NT)
            return v[:, bass.ds(g * GT, GT), :]

        @block.sync
        def _(sp):
            for g in range(NG):
                sp.dma_start(xs[:, g * GT:(g + 1) * GT, :],
                             x[:, g * GT * D:(g + 1) * GT * D].rearrange("p (t d) -> p t d", d=D))\
                  .then_inc(x_loaded[g], 16)
                if g == 0:
                    sp.dma_start(dst_b, dst_blocks).then_inc(dst_loaded, 16)
                    sp.dma_start(dst_t[:, :], dst_tiles).then_inc(dst_loaded, 16)
            for to, of in ((wn1a, Wn1[0:D, :]), (wn1b, Wn1[D:2 * D, :]), (we2, We2), (wn2, Wn2), (w1, W1), (w2, W2)):
                sp.dma_start(to[:, :], of).then_inc(params_loaded, 16)
            for q in (0, 1):
                sp.dma_start(we1[q * K_EDGE:(q + 1) * K_EDGE, :], We1).then_inc(params_loaded, 16)
            with nc.allow_non_contiguous_dma(reason="four bias columns"):
                for i, b in enumerate((be1, be2, bt, b1)):
                    sp.dma_start(cols[:, i:i + 1], b.rearrange("(p a) -> p a", a=1)).then_inc(params_loaded, 16)
            for to, b in ((bn1_r, bn1), (bn2_r, bn2), (b2_r, b2)):
                sp.dma_start(to[:, :], b.rearrange("(a d) -> a d", a=1).to_broadcast([P, D])).then_inc(params_loaded, 16)
            sp.dma_start(wt_f[:, :], Wt.to_broadcast([ZK, D])).then_inc(params_loaded, 16)
            sp.dma_start(ew_f, ew).then_inc(ew_loaded, 16)

            sp.wait_ge(base_made, 2)
            sp.dma_start(base_d.rearrange("(p j) -> p j", j=NBJ), least[:, :]).then_inc(base_stored, 16)
            sp.dma_start(great_d.rearrange("(p j) -> p j", j=NBJ), great[:, :]).then_inc(base_stored, 16)
            sp.dma_start(tleast_d.rearrange("(p j) -> p j", p=NBP), tleast[:, :, :].rearrange("p j t -> p (j t)"))\
              .then_inc(base_stored, 16)
            sp.dma_start(tgreat_d.rearrange("(p j) -> p j", p=NBP), tgreat[:, :, :].rearrange("p j t -> p (j t)"))\
              .then_inc(base_stored, 16)
            sp.wait_ge(base_stored, 64)
            one_row = base_d.rearrange("(a n) -> a n", a=1)
            great_one = great_d.rearrange("(a n) -> a n", a=1)
            sp.dma_start(great_all[:, :], great_one.to_broadcast([P, NB])).then_inc(base_loaded, 16)
            sp.dma_start(base_all[:, :], one_row.to_broadcast([P, NB])).then_inc(base_loaded, 16)

            sp.wait_ge(ew_split, 2)
            for k in range(NP3):
                for i in range(NP3):
                    sp.dma_start(ew_rows[NP3 * k + i, :].rearrange("(p c) -> p c", p=P), ew_p[:, i, :])\
                      .then_inc(ew_stored, 16)
                sp.dma_start(wt9[NP3 * k:NP3 * k + NP3, :], wt_p[NP3 * k:NP3 * k + NP3, k, :])\
                  .then_inc(wt_placed, 16)

            t0 = table0.rearrange("(p t) d -> p t d", t=NT)
            with sp.Fori(0, NG) as g:
                sp.wait_ge(nodes_made, g + 2)
                sp.dma_start(t0[:, bass.ds(g * GT, GT), :], nodes[:, bass.ds(g * GT, GT), :]).then_inc(table0_stored, 16)
            sp.wait_ge(table0_stored, 16 * NG)
            for to, of in ((tleast_all, tleast_d), (tgreat_all, tgreat_d)):
                sp.dma_start(to[0:NWIN, :], of.rearrange("(a n) -> a n", a=1).to_broadcast([NWIN, NTILE]))\
                  .then_inc(tile_ends_loaded, 16)
            sp.wait_ge(ew_stored, 16 * ZK)

            sp.wait_ge(sweeps_made, 1)
            sweeps, start, total, bodies = load_params(sp)
            ew_v = ew_rows.rearrange("k (n q c) -> k n q c", q=2, c=BLK)
            with sp.Fori(0, sweeps) as s:
                with sp.Fori(0, NBODY) as b:
                    for u in range(RING):
                        pair = b * RING + u
                        sp.wait_ge(slot_free, s * NPAIR + b * RING + u + 1)
                        sp.dma_start(idx[:, u, :], src[bass.ds(pair, 1), :, :].rearrange("a p t -> p (a t)"))\
                          .then_inc(idx_loaded[u], 16)
                        sp.dma_start(ea_s[:, u, :], ea[bass.ds(pair, 1), :, :].rearrange("a p c -> p (a c)"))\
                          .then_inc(in_loaded[u], 16)
                        sp.dma_start(ew_s[:, u, :, :], ew_v[:, bass.ds(pair, 1), :, :].rearrange("k a q c -> k (a q) c"))\
                          .then_inc(in_loaded[u], 16)

            sp.wait_ge(win_made, 1)
            sp.dma_start(win_d.rearrange("(p a) -> p a", a=1), win_i[0:NWIN, :]).then_inc(win_stored, 16)
            sp.wait_ge(win_stored, 16)
            sp.dma_start(win_row[:, :], win_d.rearrange("(a n) -> a n", a=1)).then_inc(win_loaded, 16)

            sp.wait_ge(acc_added, sweeps * NB)
            sp.dma_start(src_i, src_tiles).then_inc(src_loaded, 16)
            sp.dma_start(count_n[:, :], acc[0:1, 1, 0:N_PAD].rearrange("a (p t) -> a p t", t=NT)).then_inc(counts_moved, 16)

            t1 = table1.rearrange("(p t) d -> p t d", t=NT)
            for g in range(NG):
                sp.wait_ge(parts_made, g + 1)
                sp.dma_start(t1[:, g * GT:(g + 1) * GT, :], parts[:, g % 2].rearrange("p t i d -> p t (i d)"))\
                  .then_inc(table1_stored[g % 2], 16)

            body = sp.alloc_register("body")
            sp.reg_mov(body, 0)
            with sp.Fori(0, sweeps) as s:
                with sp.Fori(0, bodies) as b:
                    done = sp.snap(body, min_val=0, max_val=MAX_SWEEPS * NBODY)
                    for u in range(RING):
                        pair = body_at(start, b) * RING + u
                        sp.wait_ge(slot1_free, done * RING + u + 1)
                        sp.dma_start(idx[:, u, :], src[bass.ds(pair, 1), :, :].rearrange("a p t -> p (a t)"))\
                          .then_inc(idx1_loaded[u], 16)
                    sp.reg_add(body, body, 1)

            ov = out.rearrange("p (t d) -> p t d", d=D)
            with sp.Fori(0, NG) as g:
                sp.wait_ge(out_made, g + 2)
                sp.dma_start(ov[:, bass.ds(g * GT, GT), :], xs[:, bass.ds(g * GT, GT), :]).then_inc(out_stored, 16)
            sp.wait_ge(out_stored, 16 * NG)

        @block.gpsimd
        def _(pool):
            pool.memset(ident[:, :], 0.0).then_inc(consts_made, 1)
            pool.memset(ones[:, :].bitcast(F32), 1.0).then_inc(consts_made, 1)
            pool.iota(iota_s[:, :], pattern=[[1, W]], base=0, channel_multiplier=0,
                      allow_small_or_imprecise_dtypes=True).then_inc(consts_made, 1)
            for to, pattern, base, step in ((iota_b, [[1, P]], 0, 0), (iota_k, [[1, CK]], 0, 0),
                                            (blk_up, [[1, NB]], 1, 0),
                                            (win_low, [[0, 1]], 0, CW), (win_off, [[CK, NWIN]], 0, 0)):
                pool.iota(to[:, :], pattern=pattern, base=base, channel_multiplier=step,
                          allow_small_or_imprecise_dtypes=True).then_inc(consts_made, 1)
            pool.memset(zeros[:, :], 0.0).then_inc(consts_made, 1)
            pool.wait_ge(consts_made, 9)
            pool.affine_select(out=ident[:, :], in_=ident[:, :], compare_op=ALU.not_equal, fill=1.0,
                               base=0, pattern=[[-1, P]], channel_multiplier=1).then_inc(consts_made, 1)
            pool.wait_ge(sweeps_made, 1)
            sweeps, start, total, bodies = load_params(pool)

            def gathers(table, to, loaded, free, landed, times):
                with pool.Fori(0, times) as b:
                    for u in range(RING):
                        pool.wait_ge(free, b * RING + u + 1)
                        pool.wait_ge(loaded[u], b * 16 + 16)
                        pool.sem_inc(pairs_begun, 1)
                        for q in (0, 1):
                            for t in range(TB):
                                at = q * TB + t
                                pool.indirect_dma_start(
                                    to(u, q, t), None, table,
                                    bass.IndirectOffsetOnAxis(ap=idx[:, u, at:at + 1], axis=0))\
                                    .then_inc(landed[u][q], 16)

            pool.wait_ge(table0_stored, 16 * NG)
            pool.iota(tile_up, pattern=[[1, NTILE]], base=1, channel_multiplier=0,
                      allow_small_or_imprecise_dtypes=True).then_inc(tile_up_made, 1)
            gathers(table0, lambda u, q, t: rows[:, u, q, t, :], idx_loaded, slot_free, gathered, sweeps * NBODY)
            for g in range(NG):
                pool.wait_ge(normed1, g + 1)
                if g:
                    pool.wait_ge(turned1, g)
                pool.tensor_copy(stage2, nodes[:, g * GT:(g + 1) * GT, :]).then_inc(staged1, 1)
            for s in (0, 1):
                pool.wait_ge(table1_stored[s], 16 * ((NG + 1 - s) // 2))
            gathers(table1, lambda u, q, t: rows1[:, u, q, t].rearrange("p i d -> p (i d)"), idx1_loaded, slot1_free, gathered1, total)

        @block.scalar
        def _(act):
            def root(which):
                act.wait_ge(var_made, which)
                act.activation(var[:, :], var[:, :], ACT.Sqrt).then_inc(root_made, 1)

            root(1)
            act.wait_ge(stats_made, 1)
            with act.Fori(0, NG) as g:
                for u in range(GT):
                    if u == 0:
                        act.wait_ge(turned, g + 1)
                        act.wait_ge(xh_made, g + 1)
                    t = g * GT + u
                    i = act.activation(stage[:, u, :], xs[:, bass.ds(t, 1), :].rearrange("p a d -> p (a d)"), ACT.Relu,
                                       bias=shift[:, bass.ds(t, 1)], scale=rstd[:, bass.ds(t, 1)])
                i.then_inc(normed, 1)

            act.wait_ge(sweeps_made, 1)
            sweeps, start, total, bodies = load_params(act)

            def sigmoid(q, n):
                act.wait_ge(z_done, n)
                act.activation(tw[:, q, :], p_z, ACT.Sigmoid, bias=bt_c).then_inc(tw_made, 1)

            def hidden(q, n):
                act.wait_ge(hid_mm, n)
                act.activation(hid[:, q, :], p_hid[q], ACT.Relu, bias=be1_c).then_inc(hid_made, 1)

            def message(q, n):
                act.wait_ge(pre_made, n)
                m = msg[:, q, :, :].rearrange("p t d -> p (t d)")
                act.activation(m, m, ACT.Relu).then_inc(msg_made, 1)

            def pair_step(b, u, first):
                n = b * (2 * RING) + 2 * u
                if not first:
                    act.wait_ge(ef_made, n)
                sigmoid(0, n + 1)
                hidden(0, n + 1)
                if not first:
                    message(0, n - 1)
                hidden(1, n + 2)
                if not first:
                    message(1, n)
                sigmoid(1, n + 2)

            act.wait_ge(params_loaded, 16 * N_PARAMS)
            for u in range(RING):
                pair_step(0, u, u == 0)
            with act.Fori(1, sweeps * NBODY) as b:
                for u in range(RING):
                    pair_step(b, u, False)
            message(0, sweeps * NB)
            message(1, sweeps * NB)

            act.wait_ge(acc_added, sweeps * NB)
            with act.Fori(0, NG) as g:
                act.wait_ge(upd_mm, g + 1)
                act.activation(stage, acc_group(g), ACT.Copy).then_inc(acc_staged, 1)

            root(2)
            act.wait_ge(stats_made, 2)
            for g in range(NG):
                for u in range(GT):
                    t = g * GT + u
                    i = act.activation(nodes[:, t, :],
                                       xs[:, t, :], ACT.Relu,
                                       bias=shift[:, t:t + 1], scale=rstd[:, t:t + 1])
                i.then_inc(normed1, 1)
                act.wait_ge(normed1, g + 1)
                if g >= 2:
                    act.wait_ge(table1_stored[g % 2], 16 * (g // 2))
                act.activation(parts[:, g % 2, :, 0, :], nodes[:, g * GT:(g + 1) * GT, :], ACT.Copy).then_inc(parts_first, 1)

            def move_windows(k, half, windows):
                for i in windows:
                    act.wait_ge(c_built, k * CB + i + 1)
                    act.activation(c_sums[half].rearrange("p a (i n) -> p i n a", i=CB)[:, i, :, :],
                                   p_c[i % 2].rearrange("p (n a) -> p n a", a=NT), ACT.Copy).then_inc(c_moved, 1)

            def move_rows(batches):
                act.wait_ge(c_done, batches + 1)
                act.activation(c_rows[:, :], p_cs, ACT.Copy).then_inc(c_staged, 1)

            move_windows(0, 0, range(CB))
            with act.Fori(0, (NCB - 2) // 2) as kk:
                for j in (0, 1):
                    k = kk * 2 + (1 + j)
                    act.wait_ge(c_done, k)
                    move_windows(k, (1 + j) % 2, range(CB - 1))
                    move_rows(k)
                    move_windows(k, (1 + j) % 2, [CB - 1])
            act.wait_ge(c_done, NCB - 1)
            move_windows(NCB - 1, (NCB - 1) % 2, range(CB - 1))
            move_rows(NCB - 1)
            move_windows(NCB - 1, (NCB - 1) % 2, [CB - 1])
            move_rows(NCB)

            with act.Fori(0, NG) as g:
                act.wait_ge(hid2_mm, g + 1)
                act.wait_ge(out_mm, g + 1)
                act.activation(stage, p_turn, ACT.Relu, bias=b1_c).then_inc(hid2_made, 1)

        @block.tensor
        def _(pe):
            pe.wait_ge(consts_made, 10)
            pe.wait_ge(params_loaded, 16 * N_PARAMS)
            pe.sem_inc(turned, 1)
            with pe.Fori(0, NG) as g:
                pe.wait_ge(normed, g + 1)
                pe.wait_ge(stage2_made, g + 1)
                for u in range(GT):
                    i = pe.transpose(p_turn[:, u, :], stage[:, u, :], ident[:, :])
                i.then_inc(turned, 1)
                pe.wait_ge(stage2_made, g + 2)
                pe.wait_ge(nodes_made, g + 1)
                for u in range(GT):
                    i = pe.matmul(p_prod[:, u, :], stage2[:, u, :], wn1a[:, :], start=True, stop=True)
                i.then_inc(prod_made, 1)

            pe.wait_ge(sweeps_made, 1)
            sweeps, start, total, bodies = load_params(pe)
            hot_f = hot[:, :, :, :].bitcast(F32)
            def weight_product(u, q):
                pe.matmul(p_z, wt9[:, :], ew_s[:, u, q, :], start=True, stop=True).then_inc(z_done, 1)

            def hidden_product(u, q):
                k = slice(q * K_EDGE, (q + 1) * K_EDGE)
                pe.matmul(p_hid[q], we1[k, :], ea_s[k, u, :], start=True, stop=True).then_inc(hid_mm, 1)

            def edge_product(q, n):
                pe.wait_ge(hid_made, n)
                pe.matmul(p_ef[q], we2[:, :], hid[:, q, :], start=True, stop=True).then_inc(ef_mm, 1)

            def message_product(q, n):
                pe.wait_ge(ef_made, n)
                for t in range(TB):
                    i = pe.matmul(p_pre[q][:, t * D:(t + 1) * D], ef[:, q, t * P:(t + 1) * P], wn1b[:, :],
                                  start=True, stop=True)
                i.then_inc(pre_mm, 1)

            def aggregate(n):
                pe.wait_ge(msg_made, n)
                pe.wait_ge(hot_made, n)
                for q in (0, 1):
                    for t in range(TB):
                        pe.matmul(p_agg[:, q, 0, :], msg[:, q, t, :], hot_f[:, q, t, :],
                                  start=(t == 0), stop=(t == TB - 1))
                    for t in range(TB):
                        i = pe.matmul(p_agg[:, q, 1, :], ones[:, :], hot[:, q, t, :],
                                      start=(t == 0), stop=(t == TB - 1))
                i.then_inc(agg_mm, 1)

            def pair_step(b, u, first):
                n = b * (2 * RING) + 2 * u
                pe.wait_ge(in_loaded[u], b * 32 + 32)
                weight_product(u, 0)
                hidden_product(u, 0)
                hidden_product(u, 1)
                edge_product(0, n + 1)
                pe.wait_ge(tw_made, n + 1)
                weight_product(u, 1)
                edge_product(1, n + 2)
                if not first:
                    aggregate(n)
                message_product(0, n + 1)
                message_product(1, n + 2)

            pe.wait_ge(wt_placed, 16 * NP3)
            pe.wait_ge(nodes_made, NG + 1)
            for u in range(RING):
                pair_step(0, u, u == 0)
            with pe.Fori(1, sweeps * NBODY) as b:
                for u in range(RING):
                    pair_step(b, u, False)
            aggregate(sweeps * NB)

            pe.sem_inc(upd_mm, 1)
            with pe.Fori(0, NG) as g:
                pe.wait_ge(acc_staged, g + 1)
                pe.wait_ge(x1_made, g + 1)
                for u in range(GT):
                    i = pe.matmul(p_prod[:, u, :], stage[:, u, :], wn2[:, :], start=True, stop=True)
                i.then_inc(upd_mm, 1)

            with pe.Fori(0, NG) as g:
                pe.wait_ge(staged1, g + 1)
                pe.wait_ge(acc1_made, g + 1)
                for u in range(GT):
                    i = pe.transpose(p_turn[:, u, :], stage2[:, u, :], ident[:, :])
                i.then_inc(turned1, 1)

            pe.sem_inc(slot1_free, RING)
            pe.sem_inc(c_done, 1)
            pe.sem_inc(c_staged, 1)

            def sum_rows(b, u):
                n = b * (2 * RING) + 2 * u
                pe.wait_ge(hot1_made, n + 2)
                for q in (0, 1):
                    pe.wait_ge(gathered1[u][q], b * (16 * TB) + 16 * TB)
                    for t in range(TB):
                        for p in range(NP3):
                            i = pe.matmul(p_agg[:, q, 0, :], rows1[:, u, q, t, p, :], hot1[:, q, t, :],
                                          start=(t == 0 and p == 0), stop=(t == TB - 1 and p == NP3 - 1))
                i.then_inc(slot1_free, 1)

            seen = pe.alloc_register("seen")
            pe.reg_mov(seen, 0)

            def count_window(k, i):
                entry = pe.value_load(win_row[0:1, bass.ds(k + i * NCB, 1)], min_val=0, max_val=VISIT * (MAX_VISITS + 1) - 1)
                visits = nc.s_assert_within(entry // VISIT, 1, MAX_VISITS, skip_runtime_bounds_check_because="the entry's form")
                pe.wait_ge(c_moved, k * CB + i + 1)
                pe.matmul(p_c[i % 2], zeros[:, 0:P], zeros[:, :], start=True, stop=False, skip_group_check=True)
                with pe.Fori(0, visits):
                    used = pe.snap(seen, min_val=0, max_val=NWIN * MAX_VISITS * 2)
                    for h in (0, 1):
                        pe.wait_ge(c_hot, used + (h + 1))
                        for t in range(h * VH, h * VH + VH):
                            m = pe.matmul(p_c[i % 2], hot_src[:, t, :], hot_key[:, t, :], start=False, stop=True,
                                          skip_group_check=True)
                        m.then_inc(c_hot_free, 1)
                    pe.reg_add(seen, seen, 2)
                pe.matmul(p_c[i % 2], zeros[:, 0:P], zeros[:, :], start=False, stop=True, skip_group_check=True)\
                  .then_inc(c_built, 1)

            cuts = [NT * i // (CB - 1) for i in range(CB)]

            def row_sums(batches, half, i):
                if i == 0:
                    pe.wait_ge(c_moved, batches * CB + 2)
                    pe.wait_ge(c_staged, batches)
                for a in range(cuts[i], cuts[i + 1]):
                    m = pe.matmul(p_cs, c_sums[half][:, a, :], nodes[:, a, :], start=(a == 0), stop=(a == NT - 1))
                if i == CB - 2:
                    m.then_inc(c_done, 1)

            def turn_rows(batches):
                pe.wait_ge(c_staged, batches + 1)
                pe.wait_ge(c_added, batches)
                pe.sem_inc(turns_begun, 1)
                pe.transpose(p_cst, c_rows[:, :], ident[0:CROW, 0:CROW]).then_inc(c_turned, 1)

            pe.wait_ge(win_loaded, 16)
            pe.wait_ge(normed1, NG)

            def batch(k, half, first):
                for i in range(CB):
                    sum_rows(k, i)
                    if i == CB - 1 and not first:
                        turn_rows(k)
                    count_window(k, i)
                    if i < CB - 1 and not first:
                        row_sums(k, 1 - half, i)

            batch(0, 0, True)
            with pe.Fori(0, (NCB - 2) // 2) as kk:
                for j in (0, 1):
                    batch(kk * 2 + (1 + j), (1 + j) % 2, False)
            batch(NCB - 1, (NCB - 1) % 2, False)
            for i in range(CB - 1):
                row_sums(NCB, (NCB - 1) % 2, i)
            turn_rows(NCB)
            with pe.Fori(NCB, total) as b:
                for u in range(RING):
                    sum_rows(b, u)

            pe.wait_ge(acc1_added, total * (2 * RING))
            pe.sem_inc(out_mm, 1)
            with pe.Fori(0, NG) as g:
                h = acc_group(g)
                pe.wait_ge(hid2_made, g + 1)
                pe.matmul(p_turn[:, 0:4, :], w1[:, :], h[:, 0:4, :], start=True, stop=True)
                pe.matmul(p_turn[:, 4:GT, :], w1[:, :], h[:, 4:GT, :], start=True, stop=True).then_inc(hid2_mm, 1)
                pe.wait_ge(hid2_made, g + 2)
                pe.wait_ge(out_made, g + 1)
                for u in range(GT):
                    i = pe.matmul(p_prod[:, u, :], stage[:, u, :], w2[:, :], start=True, stop=True)
                i.then_inc(out_mm, 1)

        @block.vector
        def _(dve):
            step = [0]

            def chain(instruction):
                step[0] += 1
                return instruction.then_inc(dve_chain, 1)

            def settle():
                dve.wait_ge(dve_chain, step[0])

            chain(dve.memset(acc[:, :, :], 0.0))
            chain(dve.memset(stats[:, :, :], 0.0))

            dve.wait_ge(dst_loaded, 32)
            by_tile = dst_b.rearrange("p j (t c) -> p j t c", t=TB)
            chain(dve.tensor_reduce(tleast[:, :, :], by_tile, AX.X, ALU.min))
            chain(dve.tensor_reduce(tgreat[:, :, :], by_tile, AX.X, ALU.max))
            settle()
            chain(dve.tensor_reduce(least[:, :], tleast[:, :, :], AX.X, ALU.min))
            dve.tensor_reduce(great[:, :], tgreat[:, :, :], AX.X, ALU.max).then_inc(base_made, 2)

            dve.wait_ge(ew_loaded, 16)
            dve.wait_ge(params_loaded, 16 * N_PARAMS)
            for whole, pieces in ((ew_f, ew_p), (wt_f[:, :], wt_p[:, :, :])):
                for i in range(NP3):
                    last = dve.tensor_copy(pieces[:, i, :], whole)
                    if i < NP3 - 1:
                        chain(last)
                        settle()
                        chain(dve.tensor_tensor(whole, whole, pieces[:, i, :], ALU.subtract))
                        settle()
                last.then_inc(ew_split, 1)

            def layer_norm_scales(which):
                m_even, s_even, m_odd, s_odd = (stats[:, :, i] for i in (1, 2, 4, 5))
                chain(dve.tensor_tensor(mean[:, :], m_even, m_odd, ALU.add))
                chain(dve.tensor_tensor(half[:, :], m_even, m_odd, ALU.subtract))
                chain(dve.tensor_tensor(var[:, :], s_even, s_odd, ALU.add))
                settle()
                chain(dve.tensor_scalar(mean[:, :], mean[:, :], 0.5, None, ALU.mult))
                chain(dve.tensor_scalar(half[:, :], half[:, :], 0.5, None, ALU.mult))
                settle()
                chain(dve.tensor_tensor(half[:, :], half[:, :], half[:, :], ALU.mult))
                settle()
                chain(dve.scalar_tensor_tensor(out=var[:, :], in0=var[:, :], scalar=1.0 / D, in1=half[:, :],
                                               op0=ALU.mult, op1=ALU.add))
                settle()
                dve.tensor_scalar(var[:, :], var[:, :], EPS, None, ALU.add).then_inc(var_made, 1)
                dve.wait_ge(root_made, which)
                chain(dve.reciprocal(rstd[:, :], var[:, :]))
                settle()
                dve.scalar_tensor_tensor(out=shift[:, :], in0=mean[:, :], scalar=-1.0, in1=rstd[:, :],
                                         op0=ALU.mult, op1=ALU.mult).then_inc(stats_made, 1)

            for g in range(NG):
                dve.wait_ge(x_loaded[g], 16)
                for t in range(g * GT, (g + 1) * GT):
                    i = dve.bn_stats(stats[:, t, :], xs[:, t, :])
            chain(i)
            settle()
            layer_norm_scales(1)

            dve.sem_inc(stage2_made, 1)
            dve.sem_inc(nodes_made, 1)
            dve.sem_inc(xh_made, 1)
            dve.wait_ge(params_loaded, 16 * N_PARAMS)
            bn1_g = bn1_r[:, :].rearrange("p (a d) -> p a d", a=1).to_broadcast([P, GT, D])
            with dve.Fori(0, NG) as g:
                dve.wait_ge(normed, g + 1)
                dve.tensor_tensor(group(xs, g), group(xs, g), stage, ALU.add).then_inc(xh_made, 1)
                dve.wait_ge(turned, g + 2)
                dve.tensor_copy(stage2, p_turn).then_inc(stage2_made, 1)
                dve.wait_ge(prod_made, g + 1)
                dve.tensor_tensor(group(nodes, g), p_prod, bn1_g, ALU.add).then_inc(nodes_made, 1)

            dve.wait_ge(base_loaded, 32)
            chain(dve.tensor_tensor(span_row, great_all[0:1, :], base_all[0:1, :], ALU.subtract))
            chain(dve.tensor_scalar(cand_row, great_all[0:1, :], float(C_NODES), 1024.0, ALU.is_lt, ALU.mult))
            settle()
            chain(dve.tensor_tensor(cand_row, cand_row, blk_up[0:1, :], ALU.add))
            chain(dve.tensor_reduce(params[:, 0:1], span_row, AX.X, ALU.max))
            settle()
            chain(dve.tensor_scalar(cand_row, cand_row, 1.0, None, ALU.subtract))
            chain(dve.tensor_scalar(params[:, 0:1], params[:, 0:1], W_LOG2, None, ALU.logical_shift_right))
            settle()
            chain(dve.tensor_reduce(params[:, 1:2], cand_row, AX.X, ALU.min))
            chain(dve.tensor_scalar(params[:, 0:1], params[:, 0:1], 1, None, ALU.add))
            settle()
            chain(dve.tensor_scalar(params[:, 1:2], params[:, 1:2], 3, None, ALU.logical_shift_right))
            settle()
            chain(dve.tensor_scalar(params[:, 1:2], params[:, 1:2], NBODY - NCB - 1, None, ALU.min))
            settle()
            chain(dve.tensor_scalar(params[:, 3:4], params[:, 1:2], -1, NBODY, ALU.mult, ALU.add))
            settle()
            dve.tensor_tensor(params[:, 2:3], params[:, 3:4], params[:, 0:1], ALU.mult).then_inc(sweeps_made, 1)

            dve.wait_ge(sweeps_made, 1)
            sweeps, start, total, bodies = load_params(dve)

            chain(dve.tensor_copy(p_iota, iota_s[:, :]))

            def first_windows():
                chain(dve.tensor_copy(base_now[:, :], base_all[0:1, :]))
                chain(dve.tensor_tensor(rel[:, :].rearrange("p (n t) -> p n t", t=TB),
                                        dst_t[:, :].rearrange("p (n t) -> p n t", t=TB),
                                        base_all[:, :].rearrange("p (n a) -> p n a", a=1).to_broadcast([P, NB, TB]),
                                        ALU.subtract))
                settle()
                chain(dve.memset(rel[:, FULL_TILES + (TAIL > 0):NTILE], -float(2 * N_PAD)))
                if TAIL:
                    chain(dve.memset(rel[TAIL:P, FULL_TILES:FULL_TILES + 1], -float(2 * N_PAD)))
                settle()

            def next_windows(done, n):
                dve.tensor_scalar(rel[:, :], rel[:, :], float(W), None, ALU.subtract).then_inc(done, 1)
                dve.tensor_scalar(base_now[:, :], base_now[:, :], W, N_PAD, ALU.add, ALU.min).then_inc(done, 1)
                dve.wait_ge(done, n * 2 + 2)
                dve.sem_inc(windows_moved, 1)

            iota_t = p_iota.rearrange("p (a w) -> p a w", a=1).to_broadcast([P, TB, W])

            def one_hot(to, b, u, q):
                at = b * (RING * 2 * TB) + (2 * u + q) * TB
                r = rel[:, bass.ds(at, TB)].rearrange("p (t a) -> p t a", a=1).to_broadcast([P, TB, W])
                return dve.tensor_tensor(to[:, q, :, :], iota_t, r, ALU.is_equal)

            first_windows()
            dve.sem_inc(slot_free, RING)

            w = slice(0, NWIN)
            low, high, first, last, n = (win_n[w, i:i + 1] for i in range(5))
            dve.wait_ge(tile_ends_loaded, 32)
            dve.wait_ge(tile_up_made, 1)
            chain(dve.tensor_copy(low, win_low[w, :]))
            chain(dve.tensor_scalar(high, win_low[w, :], float(CW - 1), None, ALU.add))
            settle()
            chain(dve.tensor_scalar(meets[w, :], tleast_all[w, :], high, None, ALU.is_le))
            settle()
            chain(dve.scalar_tensor_tensor(out=meets[w, :], in0=tgreat_all[w, :], scalar=low, in1=meets[w, :],
                                           op0=ALU.is_ge, op1=ALU.mult))
            settle()
            chain(dve.scalar_tensor_tensor(out=firsts[w, :], in0=tile_up[w, :], scalar=-float(NTILE + 1), in1=meets[w, :],
                                           op0=ALU.add, op1=ALU.mult))
            settle()
            chain(dve.tensor_reduce(first, firsts[w, :], AX.X, ALU.min))
            chain(dve.tensor_tensor(meets[w, :], meets[w, :], tile_up[w, :], ALU.mult))
            settle()
            chain(dve.tensor_reduce(last, meets[w, :], AX.X, ALU.max))
            chain(dve.tensor_scalar(first, first, float(NTILE), None, ALU.add))
            settle()
            chain(dve.tensor_scalar(first, first, float(NTILE - 1), None, ALU.min))
            settle()
            chain(dve.tensor_tensor(n, last, first, ALU.subtract))
            settle()
            chain(dve.tensor_scalar(n, n, 1.0 / VT, 0.5 - 0.5 / VT, ALU.mult, ALU.add))
            settle()
            chain(dve.tensor_scalar(n, n, ROUND, None, ALU.add))
            settle()
            chain(dve.tensor_scalar(n, n, ROUND, None, ALU.subtract))
            settle()
            chain(dve.tensor_scalar(n, n, 1.0, float(VISIT), ALU.max, ALU.mult))
            settle()
            dve.tensor_tensor(win_i[w, :], n, first, ALU.add).then_inc(win_made, 1)

            def window_base(blk):
                return dve.value_load(base_now[0:1, bass.ds(blk, 1)], min_val=0, max_val=N_PAD)

            def add_sums(total, blk, pairs):
                starts = [window_base(blk + q) for q in (0, 1)]
                dve.wait_ge(agg_mm, pairs)
                for q, at in enumerate(starts):
                    to = acc[:, :, bass.ds(at, W)]
                    dve.wait_ge(acc_added, total + q)
                    dve.tensor_tensor(to, p_agg[:, q, :, :], to, ALU.add).then_inc(acc_added, 1)

            def pair_step(s, b, u, first):
                total = s * NB + b * (2 * RING) + 2 * u
                for q in (0, 1):
                    dve.wait_ge(ef_mm, total + q + 1)
                    dve.wait_ge(tw_made, total + q + 1)
                    dve.scalar_tensor_tensor(out=ef[:, q, :], in0=p_ef[q], scalar=be2_c, in1=tw[:, q, :],
                                             op0=ALU.add, op1=ALU.mult).then_inc(ef_made, 1)
                if not first:
                    add_sums(total - 2, b * (2 * RING) + 2 * u - 2, s * NPAIR + b * RING + u)
                for q in (0, 1):
                    one_hot(hot, b, u, q).then_inc(hot_made, 1)
                for q in (0, 1):
                    dve.wait_ge(pre_mm, total + q + 1)
                    dve.wait_ge(gathered[u][q], (s * NBODY + b) * (16 * TB) + 16 * TB)
                    dve.tensor_tensor(msg[:, q, :, :].rearrange("p t d -> p (t d)"), p_pre[q],
                                      rows[:, u, q, :, :].rearrange("p t d -> p (t d)"), ALU.add)\
                       .then_inc(pre_made, 1)
                dve.wait_ge(pre_made, total + 2)
                dve.sem_inc(slot_free, 1)

            with dve.Fori(0, sweeps) as s:
                for u in range(RING):
                    pair_step(s, 0, u, u == 0)
                with dve.Fori(1, NBODY) as b:
                    for u in range(RING):
                        pair_step(s, b, u, False)
                add_sums(s * NB + NB - 2, NB - 2, s * NPAIR + NPAIR)
                dve.wait_ge(acc_added, s * NB + NB)
                next_windows(rel_made, s)

            dve.sem_inc(x1_made, 1)
            dve.wait_ge(counts_moved, 16)
            bn2_g = bn2_r[:, :].rearrange("p (a d) -> p a d", a=1).to_broadcast([P, GT, D])
            with dve.Fori(0, NG) as g:
                c = count_n[:, bass.ds(g * GT, GT)].rearrange("p (t a) -> p t a", a=1).to_broadcast([P, GT, D])
                dve.tensor_tensor(stage2, bn2_g, c, ALU.mult).then_inc(x1_chain, 1)
                dve.wait_ge(x1_chain, g * 2 + 1)
                dve.tensor_tensor(group(xs, g), group(xs, g), stage2, ALU.add).then_inc(x1_chain, 1)
                dve.wait_ge(upd_mm, g + 2)
                dve.wait_ge(x1_chain, g * 2 + 2)
                dve.tensor_tensor(group(xs, g), group(xs, g), p_prod, ALU.add).then_inc(x1_made, 1)
                dve.wait_ge(x1_made, g + 2)
                for u in range(GT):
                    t = g * GT + u
                    i = dve.bn_stats(stats[:, bass.ds(t, 1), :].rearrange("p a s -> p (a s)"),
                                     xs[:, bass.ds(t, 1), :].rearrange("p a d -> p (a d)"))
                i.then_inc(x1_stats, 1)
            dve.wait_ge(x1_stats, NG)
            layer_norm_scales(2)

            dve.sem_inc(acc1_made, 1)
            for g in range(NG):
                dve.wait_ge(parts_first, g + 1)
                if g:
                    dve.wait_ge(parts_made, g)
                dve.tensor_tensor(left, nodes[:, g * GT:(g + 1) * GT, :], parts[:, g % 2, :, 0, :], ALU.subtract)\
                   .then_inc(parts_chain, 1)
                dve.wait_ge(parts_chain, 2 * g + 1)
                dve.tensor_copy(parts[:, g % 2, :, 1, :], left).then_inc(parts_chain, 1)
                dve.wait_ge(parts_chain, 2 * g + 2)
                dve.tensor_tensor(parts[:, g % 2, :, 2, :], left, parts[:, g % 2, :, 1, :], ALU.subtract)\
                   .then_inc(parts_made, 1)
                dve.wait_ge(turned1, g + 1)
                dve.tensor_copy(acc_group(g), p_turn).then_inc(acc1_made, 1)
            first_windows()
            dve.wait_ge(acc1_made, NG + 1)

            def add_sums1(batches, total, blk, pairs):
                starts = [window_base(blk + q) for q in (0, 1)]
                dve.wait_ge(c_added, batches)
                dve.wait_ge(slot1_free, pairs + RING)
                for q, at in enumerate(starts):
                    to = acc[:, 0, bass.ds(at, W)]
                    dve.wait_ge(acc1_added, total + q)
                    dve.tensor_tensor(to, p_agg[:, q, 0, :], to, ALU.add).then_inc(acc1_added, 1)

            def pair_hots(b, u):
                for q in (0, 1):
                    one_hot(hot1, b, u, q).then_inc(hot1_made, 1)

            def pair_sums(n, b, u, batches):
                add_sums1(batches, n * (2 * RING) + 2 * u, b * (2 * RING) + 2 * u, n * RING + u + 1)

            dve.wait_ge(src_loaded, 16)
            chain(dve.tensor_scalar(src_b, src_i, 1.0 / NT, 0.5 / NT - 0.5, ALU.mult, ALU.add))
            settle()
            chain(dve.tensor_scalar(src_b, src_b, ROUND, None, ALU.add))
            settle()
            chain(dve.tensor_scalar(src_b, src_b, ROUND, None, ALU.subtract))
            settle()
            chain(dve.scalar_tensor_tensor(out=src_t, in0=src_b, scalar=-float(NT), in1=src_i,
                                           op0=ALU.mult, op1=ALU.add))
            settle()
            chain(dve.scalar_tensor_tensor(out=key, in0=dst_t[:, :], scalar=float(NT), in1=src_t,
                                           op0=ALU.mult, op1=ALU.add))
            settle()
            chain(dve.tensor_scalar(rel_add, dst_t[:, :], float(C_NODES), -float(2 * N_PAD), ALU.is_lt, ALU.mult))
            settle()
            chain(dve.tensor_tensor(rel[:, :], rel[:, :], rel_add, ALU.add))
            chain(dve.memset(key_all[:, FULL_TILES + (TAIL > 0):NTILE + VT], -1.0))
            chain(dve.memset(src_b_all[:, NTILE:NTILE + VT], 0.0))
            if TAIL:
                chain(dve.memset(key[TAIL:P, FULL_TILES:FULL_TILES + 1], -1.0))
            settle()

            seen = dve.alloc_register("seen")
            dve.reg_mov(seen, 0)

            iota_v = iota_b[:, :].rearrange("p (a c) -> p a c", a=1).to_broadcast([P, VH, P])

            def window_hots(k, i):
                win = k + i * NCB
                entry = dve.value_load(win_row[0:1, bass.ds(win, 1)], min_val=0, max_val=VISIT * (MAX_VISITS + 1) - 1)
                first = entry % VISIT
                visits = nc.s_assert_within(entry // VISIT, 1, MAX_VISITS, skip_runtime_bounds_check_because="the entry's form")
                with dve.Fori(0, visits) as v:
                    at = nc.s_assert_within(first + v * VT, 0, NTILE - 1,
                                            skip_runtime_bounds_check_because="the last visit begins at a tile")
                    made = dve.snap(seen, min_val=0, max_val=NWIN * MAX_VISITS * 2)
                    for h in (0, 1):
                        dve.wait_ge(c_hot_free, made + (h + 1))
                        half_src = src_b_all[:, h * VH:NTILE + VT][:, bass.ds(at, VH)].rearrange("p (t a) -> p t a", a=1)
                        dve.tensor_tensor(hot_src[:, h * VH:h * VH + VH, :], iota_v, half_src.to_broadcast([P, VH, P]),
                                          ALU.is_equal)
                        for t in range(h * VH, h * VH + VH):
                            m = dve.tensor_scalar(hot_key[:, t, :], iota_k[:, :], win_off[:, bass.ds(win, 1)],
                                                  key_all[:, t:NTILE + VT][:, bass.ds(at, 1)], ALU.add, ALU.is_equal)
                        m.then_inc(c_hot, 1)
                    dve.reg_add(seen, seen, 2)

            dve.wait_ge(win_loaded, 16)
            dve.sem_inc(c_hot_free, 2)
            dve.sem_inc(c_moved, 2)
            dve.sem_inc(c_added, 1)
            acc_c = acc[:, 0, 0:C_NODES].rearrange("p (i k n) -> p k i n", k=NCB, n=CW)

            def add_rows(batches):
                dve.wait_ge(c_turned, batches)
                to = acc_c[:, bass.ds(batches - 1, 1), :, :].rearrange("p a i n -> p (a i) n")
                dve.tensor_tensor(to, p_cst.rearrange("p (i n) -> p i n", i=CB), to, ALU.add).then_inc(c_added, 1)

            def batch(k, first):
                at = body_at(start, k)
                for i in range(CB):
                    pair_hots(at, i)
                    window_hots(k, i)
                    pair_sums(k, at, i, 1 if first else k)
                if not first:
                    dve.wait_ge(acc1_added, k * (2 * RING) + 2 * RING)
                    add_rows(k)

            batch(0, True)
            with dve.Fori(1, NCB) as k:
                batch(k, False)
            dve.wait_ge(acc1_added, NCB * (2 * RING))
            add_rows(NCB)
            with dve.Fori(NCB, bodies) as b:
                for u in range(RING):
                    pair_hots(body_at(start, b), u)
                    pair_sums(b, body_at(start, b), u, NCB + 1)
            with dve.If(sweeps > 1):
                body = dve.alloc_register("body")
                dve.reg_mov(body, bodies)
                with dve.Fori(1, sweeps) as s:
                    done = dve.snap(body, min_val=0, max_val=MAX_SWEEPS * NBODY)
                    dve.wait_ge(acc1_added, done * (2 * RING))
                    next_windows(rel1_made, s - 1)
                    with dve.Fori(0, bodies) as b:
                        done = dve.snap(body, min_val=0, max_val=MAX_SWEEPS * NBODY)
                        for u in range(RING):
                            pair_hots(body_at(start, b), u)
                            pair_sums(done, body_at(start, b), u, NCB + 1)
                        dve.reg_add(body, body, 1)

            dve.sem_inc(hid2_made, 1)
            dve.sem_inc(out_made, 1)
            b2_g = b2_r[:, :].rearrange("p (a d) -> p a d", a=1).to_broadcast([P, GT, D])
            with dve.Fori(0, NG) as g:
                dve.wait_ge(out_mm, g + 2)
                dve.tensor_tensor(stage2, p_prod, b2_g, ALU.add).then_inc(out_chain, 1)
                dve.wait_ge(out_chain, g + 1)
                dve.scalar_tensor_tensor(out=group(xs, g), in0=stage2, scalar=0.0, in1=group(xs, g),
                                         op0=ALU.max, op1=ALU.add).then_inc(out_made, 1)


def kernel(x, src, dst, edge_attr_64, edge_weight, **w):
    import numpy as np
    import concourse.bacc as bacc
    from concourse.bass_utils import run_bass_kernel_spmd

    x, src, dst, ea, ew = (np.asarray(a) for a in (x, src, dst, edge_attr_64, edge_weight))
    extra = E_PAD - N_EDGES
    src = np.pad(src, (0, extra))
    dst = np.pad(dst, (0, extra), mode="edge")
    ea = np.pad(ea, ((0, extra), (0, 0)))
    arrays = {
        "x": np.pad(x, ((0, N_PAD - N_NODES), (0, 0))).reshape(P, NT * D),
        "ea": ea.reshape(NPAIR, 2, BLK, K_EDGE).transpose(0, 1, 3, 2).reshape(NPAIR, P, BLK),
        "ew": np.pad(ew, (0, extra)).reshape(P, E_PAD // P),
        "src": src.reshape(NPAIR, 2 * TB, P).transpose(0, 2, 1),
        "src_tiles": src.reshape(NTILE, P).T,
        "dst_tiles": dst.reshape(NTILE, P).T,
        "dst_blocks": dst.reshape(NBP, NBJ, BLK),
    }
    names = {"We1": "L0_gnn_We1", "be1": "L0_gnn_be1", "We2": "L0_gnn_We2", "be2": "L0_gnn_be2", "Wt": "L0_gnn_Wt",
             "bt": "L0_gnn_bt", "Wn1": "L0_gnn_Wn1", "bn1": "L0_gnn_bn1", "Wn2": "L0_gnn_Wn2", "bn2": "L0_gnn_bn2",
             "W1": "L1_gnn_W1", "b1": "L1_gnn_b1", "W2": "L1_gnn_W2", "b2": "L1_gnn_b2"}
    for short, name in names.items():
        arrays[short] = np.asarray(w[name])
    arrays = {k: np.ascontiguousarray(a) for k, a in arrays.items()}
    nc = bacc.Bacc("TRN2", target_bir_lowering=False, num_devices=1)
    args = {k: nc.dram_tensor(f"in_{k}", a.shape, mybir.dt.from_np(a.dtype), kind="ExternalInput").ap()
            for k, a in arrays.items()}
    out = nc.dram_tensor("out", (P, NT * D), F32, kind="ExternalOutput").ap()
    gnn_program(nc, **args, out=out)
    r = run_bass_kernel_spmd(nc, [{f"in_{k}": a for k, a in arrays.items()}], core_ids=[0])
    return r.results[0]["out"].reshape(N_PAD, D)[:N_NODES]
```

```python
from contextlib import ExitStack

import concourse.bass as bass
from concourse import mybir

F32 = mybir.dt.float32
F32R = mybir.dt.float32r
BF16 = mybir.dt.bfloat16
F16 = mybir.dt.float16
I32 = mybir.dt.int32
ALU = mybir.AluOpType
ACT = mybir.ActivationFunctionType
AX = mybir.AxisListType

P = 128
D = 128
K_EDGE = 64
N_NODES = 6250
N_EDGES = 200000
EPS = 1e-5

NT = -(-N_NODES // P)
GT = 7
NG = NT // GT
N_PAD = NT * P
assert NG * GT == NT

TB = 4
BLK = TB * P
RING = 4
NPAIR = -(-N_EDGES // (2 * BLK * RING)) * RING
NBODY = NPAIR // RING
NB = 2 * NPAIR
NTILE = NB * TB
E_PAD = NTILE * P

W_LOG2 = 6
W = 1 << W_LOG2
ACC = N_PAD + W
NBP = 98
NBJ = NB // NBP
assert NBP * NBJ == NB
MAX_SWEEPS = N_PAD // W + 1
FULL_TILES = N_EDGES // P
TAIL = N_EDGES % P
assert TAIL in (0, 32, 64, 96)

CW = 10
CK = CW * NT
VTS = (8, 8, 6, 6, 6)
VT = max(VTS)
VH = VT // 2
CB = 5
NCB = 26
NWIN = CB * NCB
NH = NWIN // 2
C_NODES = NWIN * CW
assert CB > RING and NCB % 2 == 0 and CK <= 512 and NWIN % 2 == 0 and NH <= P and NCB < NBODY
ROUND = 1.5 * 2.0 ** 23
VISIT = 2048
MAX_VISITS = -(-NTILE // min(VTS))
assert len(VTS) == CB and all(v % 2 == 0 for v in VTS) and NTILE < VISIT and VISIT * (NTILE + 1) < 2 ** 24

NP3 = 3
ZK = NP3 * NP3


def gnn_program(nc, x, ea, ew, src, src_tiles, dst_tiles, dst_blocks, We1, be1, We2, be2, Wt, bt, Wn1, bn1, Wn2, bn2,
                W1, b1, W2, b2, out):
    ctx = ExitStack()
    with ctx:
        def sb(name, shape, dt=F32):
            return ctx.enter_context(nc.sbuf_tensor(name, shape, dt))

        def sem(name):
            return ctx.enter_context(nc.semaphore(name))

        def dram(name, shape, dt=F32):
            return nc.dram_tensor(name, shape, dt, kind="Internal").ap()

        table0 = dram("table0", (N_PAD, D))
        table1 = dram("table1", (N_PAD, NP3 * D), BF16)
        ew_rows = dram("ew_rows", (ZK, E_PAD), BF16)
        base_d = dram("base_d", (NB,), I32)
        great_d = dram("great_d", (NB,), I32)
        tleast_d = dram("tleast_d", (NTILE,), I32)
        tgreat_d = dram("tgreat_d", (NTILE,), I32)
        win_d = dram("win_d", (NWIN,), I32)

        xs = sb("xs", [P, NT, D])
        nodes = sb("nodes", [P, NT, D])
        acc = sb("acc", [P, 2, ACC])
        stats = sb("stats", [P, NT, 6])
        mean = sb("mean", [P, NT])
        half = sb("half", [P, NT])
        var = sb("var", [P, NT])
        rstd = sb("rstd", [P, NT])
        count_n = sb("count_n", [P, NT])
        shift = sb("shift", [P, NT])

        we1 = sb("we1", [P, D])
        we2 = sb("we2", [P, D])
        wn1a = sb("wn1a", [P, D])
        wn1b = sb("wn1b", [P, D])
        wn2 = sb("wn2", [P, D])
        w1 = sb("w1", [P, D])
        w2 = sb("w2", [P, D])
        cols = sb("cols", [P, 4])
        be1_c, be2_c, bt_c, b1_c = (cols[:, i:i + 1] for i in range(4))
        bn1_r = sb("bn1_r", [P, D])
        bn2_r = sb("bn2_r", [P, D])
        b2_r = sb("b2_r", [P, D])
        wt_f = sb("wt_f", [ZK, D])
        wt_p = sb("wt_p", [ZK, NP3, D], BF16)
        wt9 = sb("wt9", [ZK, D], BF16)
        ones = sb("ones", [P, 1], F32R)
        iota_s = sb("iota_s", [P, W])

        EC = E_PAD // P
        CROW = CB * CW
        HOT = VT * (P + CK) // 2
        sizes = [EC, NP3 * EC // 2, RING * BLK, RING * BLK, 2 * BLK]
        arena = sb("arena", [P, max(sum(sizes), 2 * (NTILE + VT) + 2 * NT * CROW + HOT)])
        cuts = [sum(sizes[:i]) for i in range(len(sizes) + 1)]
        ew_f, ew_p, ea_s, ew_s, hid = (arena[:, a:b] for a, b in zip(cuts, cuts[1:]))
        ew_p = ew_p.bitcast(BF16).rearrange("p (i c) -> p i c", i=NP3)
        ea_s = ea_s.rearrange("p (u c) -> p u c", u=RING)
        ew_s = ew_s[0:ZK, :].bitcast(BF16).rearrange("p (u q c) -> p u q c", u=RING, q=2)
        hid = hid.rearrange("p (q c) -> p q c", q=2)
        src_b_all, key_all = (arena[:, i * (NTILE + VT):(i + 1) * (NTILE + VT)] for i in range(2))
        src_b, key = src_b_all[:, 0:NTILE], key_all[:, 0:NTILE]
        at = 2 * (NTILE + VT)
        src_t, rel_add = (arena[:, at + i * NTILE:at + (i + 1) * NTILE] for i in range(2))
        src_i = rel_add.bitcast(I32)
        c_sums = [arena[:, at + j * NT * CROW:at + (j + 1) * NT * CROW].rearrange("p (a n) -> p a n", a=NT) for j in (0, 1)]
        at += 2 * NT * CROW
        hot_src = arena[:, at:at + VT * P // 2].bitcast(BF16).rearrange("p (t c) -> p t c", t=VT)
        at += VT * P // 2
        hot_key = arena[:, at:at + VT * CK // 2].bitcast(BF16).rearrange("p (t c) -> p t c", t=VT)
        c_rows = sb("c_rows", [CROW, D])
        dst_t = sb("dst_t", [P, NTILE], I32)
        least = sb("least", [NBP, NBJ], I32)
        great = sb("great", [NBP, NBJ], I32)
        base_all = sb("base_all", [P, NB], I32)
        base_now = sb("base_now", [1, NB], I32)
        great_all = sb("great_all", [P, NB], I32)
        params = sb("params", [1, 4], I32)
        blk_up = sb("blk_up", [1, NB])
        tleast = sb("tleast", [NBP, NBJ, TB], I32)
        tgreat = sb("tgreat", [NBP, NBJ, TB], I32)
        win_low = sb("win_low", [P, 1])
        win_n = sb("win_n", [P, 5])
        win_i = sb("win_i", [P, 2], I32)
        win_row = sb("win_row", [1, NWIN], I32)
        win_off = sb("win_off", [P, NWIN])
        iota_b = sb("iota_b", [P, P], F16)
        iota_k = sb("iota_k", [P, CK], F16)
        zeros = sb("zeros", [1, CK], BF16)
        rel = sb("rel", [P, NTILE])
        idx = sb("idx", [P, RING, 2 * TB], I32)
        RROW = RING * 2 * TB * D
        big = sb("big", [P, RROW * NP3 // 2])
        assert RROW * NP3 // 2 == RROW + 2 * TB * D + 2 * BLK
        rows = big[:, 0:RROW].rearrange("p (u q t d) -> p u q t d", u=RING, q=2, t=TB)
        msg_flat = big[:, RROW:RROW + 2 * TB * D]
        msg = msg_flat.rearrange("p (q t d) -> p q t d", q=2, t=TB)
        tw = big[:, RROW + 2 * TB * D:RROW + 2 * TB * D + 2 * BLK].rearrange("p (q c) -> p q c", q=2)
        rows1 = big[:, :].bitcast(BF16).rearrange("p (u q t i d) -> p u q t i d", u=RING, q=2, t=TB, i=NP3)
        parts = big[:, 0:2 * GT * D * NP3 // 2].bitcast(BF16).rearrange("p (s t i d) -> p s t i d", s=2, t=GT, i=NP3)
        left = big[:, GT * D * NP3:GT * D * NP3 + GT * D].rearrange("p (t d) -> p t d", t=GT)
        ef = sb("ef", [P, 2, BLK])
        half_at = RROW + 2 * TB * D - GT * D
        stages, stages2 = ([a[:, 0:GT * D].rearrange("p (t d) -> p t d", t=GT) for a in pair] for pair in (
            (big[:, RROW + 2 * TB * D:], big[:, half_at:]),
            (ef[:, :, :].rearrange("p q c -> p (q c)"), big[:, half_at - GT * D:])))
        assert NBJ * BLK + 2 * NB <= half_at - GT * D and GT * D * (NP3 + 1) <= RROW + 2 * TB * D
        dst_b = big[0:NBP, 0:NBJ * BLK].bitcast(I32).rearrange("p (j c) -> p j c", j=NBJ)
        cand_row, span_row = big[0:1, NBJ * BLK:NBJ * BLK + NB], big[0:1, NBJ * BLK + NB:NBJ * BLK + 2 * NB].bitcast(I32)
        nodes_flat = nodes[:, :, :].rearrange("p t d -> p (t d)")
        tleast_all, tgreat_all = (nodes_flat[:, i * NTILE:(i + 1) * NTILE].bitcast(I32) for i in (0, 1))
        meets, firsts = (nodes_flat[:, i * NTILE:(i + 1) * NTILE] for i in (2, 3))
        tile_up = ew_f
        assert 4 * NTILE <= NT * D and NTILE == EC
        hot = sb("hot", [P, 2, TB, W], F32R)
        hot1 = sb("hot1", [P, 2, TB, W], BF16)

        BANK = 512
        ps = ctx.enter_context(nc.psum_tensor("ps", [P, 8 * BANK], F32))
        p_hid = [ps[:, q * BANK:(q + 1) * BANK] for q in (0, 1)]
        p_z = ps[:, 2 * BANK:3 * BANK]
        p_ef = [ps[:, q * BANK:(q + 1) * BANK] for q in (3, 4)]
        p_pre = [ps[:, q * BANK:(q + 1) * BANK] for q in (5, 6)]
        p_agg = ps[:, 7 * BANK:7 * BANK + 4 * W].rearrange("p (q s w) -> p q s w", q=2, s=2)
        p_iota = ps[:, 7 * BANK + 4 * W:7 * BANK + 5 * W]
        p_c = [ps[:, q * BANK:q * BANK + CK] for q in (0, 1)]
        p_cs = ps[0:CROW, 2 * BANK:2 * BANK + D]
        p_cst = ps[:, 3 * BANK:3 * BANK + CROW]
        p_turn, p_prod = ([ps[:, q * BANK:q * BANK + GT * D].rearrange("p (t d) -> p t d", t=GT) for q in pair]
                          for pair in ((0, 4), (2, 6)))

        ident = sb("ident", [P, P])

        x_loaded = [sem(f"x_loaded{g}") for g in range(NG)]
        params_loaded = sem("params_loaded")
        dst_loaded = sem("dst_loaded")
        dst_tiles_loaded = sem("dst_tiles_loaded")
        ew_loaded = sem("ew_loaded")
        consts_made = sem("consts_made")
        base_made = sem("base_made")
        base_stored = sem("base_stored")
        base_loaded = sem("base_loaded")
        sweeps_made = sem("sweeps_made")
        ew_split = sem("ew_split")
        ew_stored = sem("ew_stored")
        wt_placed = sem("wt_placed")
        pool_chain = sem("pool_chain")
        dve_chain = sem("dve_chain")
        var_made = sem("var_made")
        root_made = sem("root_made")
        stats_made = sem("stats_made")
        normed = sem("normed")
        turned = sem("turned")
        stage2_made = sem("stage2_made")
        prod_made = sem("prod_made")
        nodes_made = sem("nodes_made")
        xh_made = sem("xh_made")
        table0_stored = sem("table0_stored")
        table1_stored = [sem(f"table1_stored{s}") for s in (0, 1)]

        in_loaded = [sem(f"in_loaded{u}") for u in range(RING)]
        idx_loaded = [sem(f"idx_loaded{u}") for u in range(RING)]
        gathered = [[sem(f"gathered{u}{q}") for q in (0, 1)] for u in range(RING)]
        pairs_begun = sem("pairs_begun")
        slot_free = sem("slot_free")
        z_done = sem("z_done")
        hid_mm = sem("hid_mm")
        ef_mm = sem("ef_mm")
        pre_mm = sem("pre_mm")
        agg_mm = sem("agg_mm")
        tw_made = sem("tw_made")
        hid_made = sem("hid_made")
        ef_made = sem("ef_made")
        pre_made = sem("pre_made")
        msg_made = sem("msg_made")
        acc_added = sem("acc_added")
        hot_made = sem("hot_made")
        rel_made = sem("rel_made")
        rel1_made = sem("rel1_made")
        windows_moved = sem("windows_moved")
        x1_stats = sem("x1_stats")
        out_chain = sem("out_chain")

        acc_staged = sem("acc_staged")
        counts_moved = sem("counts_moved")
        x1_chain = sem("x1_chain")
        acc_zeroed = sem("acc_zeroed")
        upd_mm = sem("upd_mm")
        x1_made = sem("x1_made")
        normed1 = sem("normed1")
        staged1 = sem("staged1")
        turned1 = sem("turned1")
        acc1_made = sem("acc1_made")

        idx1_loaded = [sem(f"idx1_loaded{u}") for u in range(RING)]
        gathered1 = [[sem(f"gathered1{u}{q}") for q in (0, 1)] for u in range(RING)]
        slot1_free = sem("slot1_free")
        hot1_made = sem("hot1_made")
        acc1_added = sem("acc1_added")

        tile_ends_loaded = sem("tile_ends_loaded")
        tile_up_made = sem("tile_up_made")
        win_made = sem("win_made")
        win_stored = sem("win_stored")
        win_loaded = sem("win_loaded")
        src_loaded = sem("src_loaded")
        c_hot = sem("c_hot")
        c_hot_free = sem("c_hot_free")
        turns_begun = sem("turns_begun")
        c_built = sem("c_built")
        c_moved = sem("c_moved")
        c_done = sem("c_done")
        c_staged = sem("c_staged")
        c_turned = sem("c_turned")
        parts_first = sem("parts_first")
        parts_chain = sem("parts_chain")
        parts_made = sem("parts_made")
        c_added = sem("c_added")

        hid2_mm = sem("hid2_mm")
        hid2_made = sem("hid2_made")
        out_mm = sem("out_mm")
        out_made = sem("out_made")
        out_stored = sem("out_stored")

        N_PARAMS = 16
        block = ctx.enter_context(nc.Block())

        def load_params(engine):
            return (engine.value_load(params[0:1, 0:1], min_val=1, max_val=MAX_SWEEPS),
                    engine.value_load(params[0:1, 1:2], min_val=0, max_val=NBODY - NCB - 1),
                    engine.value_load(params[0:1, 2:3], min_val=NCB + 1, max_val=MAX_SWEEPS * NBODY),
                    engine.value_load(params[0:1, 3:4], min_val=NCB + 1, max_val=NBODY))

        def body_at(start, b):
            return nc.s_assert_within(start + b, 0, NBODY - 1,
                                      skip_runtime_bounds_check_because="b ends at NBODY - start")

        def group(ap, g):
            return ap[:, bass.ds(g * GT, GT)]

        def acc_group(g, which=0):
            v = acc[:, which, 0:N_PAD].rearrange("f (p t) -> f t p", t=NT)
            return v[:, bass.ds(g * GT, GT), :]

        @block.sync
        def _(sp):
            sp.dma_start(dst_b, dst_blocks).then_inc(dst_loaded, 16)
            for g in range(NG):
                sp.dma_start(xs[:, g * GT:(g + 1) * GT, :],
                             x[:, g * GT * D:(g + 1) * GT * D].rearrange("p (t d) -> p t d", d=D))\
                  .then_inc(x_loaded[g], 16)
                if g == 0:
                    sp.dma_start(ew_f, ew).then_inc(ew_loaded, 16)
                    sp.dma_start(dst_t[:, :], dst_tiles).then_inc(dst_tiles_loaded, 16)
            for to, of in ((wn1a, Wn1[0:D, :]), (wn1b, Wn1[D:2 * D, :]), (we2, We2), (wn2, Wn2), (w1, W1), (w2, W2)):
                sp.dma_start(to[:, :], of).then_inc(params_loaded, 16)
            for q in (0, 1):
                sp.dma_start(we1[q * K_EDGE:(q + 1) * K_EDGE, :], We1).then_inc(params_loaded, 16)
            with nc.allow_non_contiguous_dma(reason="four bias columns"):
                for i, b in enumerate((be1, be2, bt, b1)):
                    sp.dma_start(cols[:, i:i + 1], b.rearrange("(p a) -> p a", a=1)).then_inc(params_loaded, 16)
            for to, b in ((bn1_r, bn1), (bn2_r, bn2), (b2_r, b2)):
                sp.dma_start(to[:, :], b.rearrange("(a d) -> a d", a=1).to_broadcast([P, D])).then_inc(params_loaded, 16)
            sp.dma_start(wt_f[:, :], Wt.to_broadcast([ZK, D])).then_inc(params_loaded, 16)

            sp.wait_ge(base_made, 2)
            sp.dma_start(base_d.rearrange("(p j) -> p j", j=NBJ), least[:, :]).then_inc(base_stored, 16)
            sp.dma_start(great_d.rearrange("(p j) -> p j", j=NBJ), great[:, :]).then_inc(base_stored, 16)
            sp.dma_start(tleast_d.rearrange("(p j) -> p j", p=NBP), tleast[:, :, :].rearrange("p j t -> p (j t)"))\
              .then_inc(base_stored, 16)
            sp.dma_start(tgreat_d.rearrange("(p j) -> p j", p=NBP), tgreat[:, :, :].rearrange("p j t -> p (j t)"))\
              .then_inc(base_stored, 16)
            sp.wait_ge(base_stored, 64)
            one_row = base_d.rearrange("(a n) -> a n", a=1)
            great_one = great_d.rearrange("(a n) -> a n", a=1)
            sp.dma_start(great_all[:, :], great_one.to_broadcast([P, NB])).then_inc(base_loaded, 16)
            sp.dma_start(base_all[:, :], one_row.to_broadcast([P, NB])).then_inc(base_loaded, 16)


            sp.wait_ge(ew_split, 2)
            for k in range(NP3):
                for i in range(NP3):
                    sp.dma_start(ew_rows[NP3 * k + i, :].rearrange("(p c) -> p c", p=P), ew_p[:, i, :])\
                      .then_inc(ew_stored, 16)
                sp.dma_start(wt9[NP3 * k:NP3 * k + NP3, :], wt_p[NP3 * k:NP3 * k + NP3, k, :])\
                  .then_inc(wt_placed, 16)

            sp.wait_ge(sweeps_made, 1)
            sweeps, start, total, bodies = load_params(sp)

            t0 = table0.rearrange("(p t) d -> p t d", t=NT)
            with sp.Fori(0, NG) as g:
                sp.wait_ge(nodes_made, g + 1)
                sp.dma_start(t0[:, bass.ds(g * GT, GT), :], nodes[:, bass.ds(g * GT, GT), :]).then_inc(table0_stored, 16)
            sp.wait_ge(ew_stored, 16 * ZK)
            sp.wait_ge(table0_stored, 16 * NG)
            for to, of in ((tleast_all, tleast_d), (tgreat_all, tgreat_d)):
                sp.dma_start(to[0:NH, :], of.rearrange("(a n) -> a n", a=1).to_broadcast([NH, NTILE]))\
                  .then_inc(tile_ends_loaded, 16)

            ew_v = ew_rows.rearrange("k (n q c) -> k n q c", q=2, c=BLK)
            with sp.Fori(0, sweeps) as s:
                with sp.Fori(0, NBODY) as b:
                    for u in range(RING):
                        pair = b * RING + u
                        sp.wait_ge(slot_free, s * NPAIR + b * RING + u + 1)
                        sp.dma_start(idx[:, u, :], src[bass.ds(pair, 1), :, :].rearrange("a p t -> p (a t)"))\
                          .then_inc(idx_loaded[u], 16)
                        sp.dma_start(ea_s[:, u, :], ea[bass.ds(pair, 1), :, :].rearrange("a p c -> p (a c)"))\
                          .then_inc(in_loaded[u], 16)
                        sp.dma_start(ew_s[:, u, :, :], ew_v[:, bass.ds(pair, 1), :, :].rearrange("k a q c -> k (a q) c"))\
                          .then_inc(in_loaded[u], 16)

            sp.wait_ge(win_made, 2)
            for h in (0, 1):
                sp.dma_start(win_d[h * NH:(h + 1) * NH].rearrange("(p a) -> p a", a=1), win_i[0:NH, h:h + 1])\
                  .then_inc(win_stored, 16)
            sp.wait_ge(win_stored, 32)
            sp.dma_start(win_row[:, :], win_d.rearrange("(a n) -> a n", a=1)).then_inc(win_loaded, 16)

            sp.wait_ge(acc_added, sweeps * NB)
            sp.dma_start(count_n[:, :], acc[0:1, 1, 0:N_PAD].rearrange("a (p t) -> a p t", t=NT)).then_inc(counts_moved, 16)
            sp.dma_start(src_i, src_tiles).then_inc(src_loaded, 16)

            t1 = table1.rearrange("(p t) d -> p t d", t=NT)
            for g in range(NG):
                sp.wait_ge(parts_made, g + 1)
                sp.dma_start(t1[:, g * GT:(g + 1) * GT, :], parts[:, g % 2].rearrange("p t i d -> p t (i d)"))\
                  .then_inc(table1_stored[g % 2], 16)

            body = sp.alloc_register("body")
            sp.reg_mov(body, 0)
            with sp.Fori(0, sweeps) as s:
                with sp.Fori(0, bodies) as b:
                    done = sp.snap(body, min_val=0, max_val=MAX_SWEEPS * NBODY)
                    for u in range(RING):
                        pair = body_at(start, b) * RING + u
                        sp.wait_ge(slot1_free, done * RING + u + 1)
                        sp.dma_start(idx[:, u, :], src[bass.ds(pair, 1), :, :].rearrange("a p t -> p (a t)"))\
                          .then_inc(idx1_loaded[u], 16)
                    sp.reg_add(body, body, 1)

            ov = out.rearrange("p (t d) -> p t d", d=D)
            with sp.Fori(0, NG) as g:
                sp.wait_ge(out_made, g + 1)
                sp.dma_start(ov[:, bass.ds(g * GT, GT), :], xs[:, bass.ds(g * GT, GT), :]).then_inc(out_stored, 16)
            sp.wait_ge(out_stored, 16 * NG)

        @block.gpsimd
        def _(pool):
            pool.memset(ident[:, :], 0.0).then_inc(consts_made, 1)
            pool.memset(ones[:, :].bitcast(F32), 1.0).then_inc(consts_made, 1)
            pool.iota(iota_s[:, :], pattern=[[1, W]], base=0, channel_multiplier=0,
                      allow_small_or_imprecise_dtypes=True).then_inc(consts_made, 1)
            for to, pattern, base, step in ((iota_b, [[1, P]], 0, 0), (iota_k, [[1, CK]], 0, 0),
                                            (blk_up, [[1, NB]], 1, 0),
                                            (win_low, [[0, 1]], 0, CW), (win_off, [[CK, NWIN]], 0, 0)):
                pool.iota(to[:, :], pattern=pattern, base=base, channel_multiplier=step,
                          allow_small_or_imprecise_dtypes=True).then_inc(consts_made, 1)
            pool.memset(zeros[:, :], 0.0).then_inc(consts_made, 1)
            pool.wait_ge(consts_made, 9)
            pool.affine_select(out=ident[:, :], in_=ident[:, :], compare_op=ALU.not_equal, fill=1.0,
                               base=0, pattern=[[-1, P]], channel_multiplier=1).then_inc(consts_made, 1)

            pool.wait_ge(ew_loaded, 16)
            n = 0
            for whole, pieces in ((ew_f, ew_p), (wt_f[:, :], wt_p[:, :, :])):
                if n:
                    pool.wait_ge(params_loaded, 16 * N_PARAMS)
                for i in range(NP3):
                    last = pool.tensor_copy(pieces[:, i, :], whole)
                    if i < NP3 - 1:
                        last.then_inc(pool_chain, 1)
                        pool.wait_ge(pool_chain, n + 1)
                        pool.tensor_tensor(whole, whole, pieces[:, i, :], ALU.subtract).then_inc(pool_chain, 1)
                        pool.wait_ge(pool_chain, n + 2)
                        n += 2
                last.then_inc(ew_split, 1)
            pool.wait_ge(ew_split, 2)
            pool.iota(tile_up, pattern=[[1, NTILE]], base=1, channel_multiplier=0,
                      allow_small_or_imprecise_dtypes=True).then_inc(tile_up_made, 1)
            pool.memset(acc[:, :, :], 0.0).then_inc(acc_zeroed, 1)

            pool.wait_ge(sweeps_made, 1)
            sweeps, start, total, bodies = load_params(pool)

            def gathers(table, to, loaded, free, landed, times):
                with pool.Fori(0, times) as b:
                    for u in range(RING):
                        pool.wait_ge(free, b * RING + u + 1)
                        pool.wait_ge(loaded[u], b * 16 + 16)
                        pool.sem_inc(pairs_begun, 1)
                        for q in (0, 1):
                            for t in range(TB):
                                at = q * TB + t
                                pool.indirect_dma_start(
                                    to(u, q, t), None, table,
                                    bass.IndirectOffsetOnAxis(ap=idx[:, u, at:at + 1], axis=0))\
                                    .then_inc(landed[u][q], 16)

            pool.wait_ge(table0_stored, 16 * NG)
            gathers(table0, lambda u, q, t: rows[:, u, q, t, :], idx_loaded, slot_free, gathered, sweeps * NBODY)
            for g in range(NG):
                pool.wait_ge(normed1, g + 1)
                if g >= 2:
                    pool.wait_ge(turned1, g - 1)
                pool.tensor_copy((stages2[0], stages[0])[g % 2], nodes[:, g * GT:(g + 1) * GT, :]).then_inc(staged1, 1)
            for s in (0, 1):
                pool.wait_ge(table1_stored[s], 16 * ((NG + 1 - s) // 2))
            gathers(table1, lambda u, q, t: rows1[:, u, q, t].rearrange("p i d -> p (i d)"), idx1_loaded, slot1_free,
                    gathered1, total)

        @block.scalar
        def _(act):
            def root(which):
                act.wait_ge(var_made, which)
                act.activation(var[:, :], var[:, :], ACT.Sqrt).then_inc(root_made, 1)

            root(1)
            act.wait_ge(stats_made, 1)
            for g in range(NG):
                if g >= 2:
                    act.wait_ge(turned, g - 1)
                    act.wait_ge(xh_made, g - 1)
                for t in range(g * GT, (g + 1) * GT):
                    i = act.activation(stages[g % 2][:, t - g * GT, :], xs[:, t, :], ACT.Relu,
                                       bias=shift[:, t:t + 1], scale=rstd[:, t:t + 1])
                i.then_inc(normed, 1)

            act.wait_ge(sweeps_made, 1)
            sweeps, start, total, bodies = load_params(act)

            def sigmoid(q, n):
                act.wait_ge(z_done, n)
                act.activation(tw[:, q, :], p_z, ACT.Sigmoid, bias=bt_c).then_inc(tw_made, 1)

            def hidden(q, n):
                act.wait_ge(hid_mm, n)
                act.activation(hid[:, q, :], p_hid[q], ACT.Relu, bias=be1_c).then_inc(hid_made, 1)

            def message(q, n):
                act.wait_ge(pre_made, n)
                m = msg[:, q, :, :].rearrange("p t d -> p (t d)")
                act.activation(m, m, ACT.Relu).then_inc(msg_made, 1)

            def pair_step(b, u, first):
                n = b * (2 * RING) + 2 * u
                if not first:
                    act.wait_ge(ef_made, n)
                sigmoid(0, n + 1)
                hidden(0, n + 1)
                if not first:
                    message(0, n - 1)
                hidden(1, n + 2)
                if not first:
                    message(1, n)
                sigmoid(1, n + 2)

            act.wait_ge(params_loaded, 16 * N_PARAMS)
            for u in range(RING):
                pair_step(0, u, u == 0)
            with act.Fori(1, sweeps * NBODY) as b:
                for u in range(RING):
                    pair_step(b, u, False)
            message(0, sweeps * NB)
            message(1, sweeps * NB)

            act.wait_ge(acc_added, sweeps * NB)
            for g in range(NG):
                if g >= 2:
                    act.wait_ge(upd_mm, g - 1)
                act.activation(stages[g % 2], acc_group(g), ACT.Copy).then_inc(acc_staged, 1)

            root(2)
            act.wait_ge(stats_made, 2)
            for g in range(NG):
                for u in range(GT):
                    t = g * GT + u
                    i = act.activation(nodes[:, t, :],
                                       xs[:, t, :], ACT.Relu,
                                       bias=shift[:, t:t + 1], scale=rstd[:, t:t + 1])
                i.then_inc(normed1, 1)
                act.wait_ge(normed1, g + 1)
                if g >= 2:
                    act.wait_ge(table1_stored[g % 2], 16 * (g // 2))
                act.activation(parts[:, g % 2, :, 0, :], nodes[:, g * GT:(g + 1) * GT, :], ACT.Copy).then_inc(parts_first, 1)

            def move_windows(k, half, windows):
                for i in windows:
                    act.wait_ge(c_built, k * CB + i + 1)
                    act.activation(c_sums[half].rearrange("p a (i n) -> p i n a", i=CB)[:, i, :, :],
                                   p_c[(half * CB + i) % 2].rearrange("p (n a) -> p n a", a=NT), ACT.Copy).then_inc(c_moved, 1)

            def move_rows(batches):
                act.wait_ge(c_done, batches + 1)
                act.activation(c_rows[:, :], p_cs, ACT.Copy).then_inc(c_staged, 1)

            move_windows(0, 0, range(CB))
            with act.Fori(0, (NCB - 2) // 2) as kk:
                for j in (0, 1):
                    k = kk * 2 + (1 + j)
                    act.wait_ge(c_done, k)
                    move_windows(k, (1 + j) % 2, range(CB - 1))
                    move_rows(k)
                    move_windows(k, (1 + j) % 2, [CB - 1])
            act.wait_ge(c_done, NCB - 1)
            move_windows(NCB - 1, (NCB - 1) % 2, range(CB - 1))
            move_rows(NCB - 1)
            move_windows(NCB - 1, (NCB - 1) % 2, [CB - 1])
            move_rows(NCB)

            for g in range(NG):
                act.wait_ge(hid2_mm, g + 1)
                if g >= 2:
                    act.wait_ge(out_mm, g - 1)
                act.activation(stages[g % 2], p_turn[g % 2], ACT.Relu, bias=b1_c).then_inc(hid2_made, 1)

        @block.tensor
        def _(pe):
            pe.wait_ge(consts_made, 10)
            pe.wait_ge(params_loaded, 16 * N_PARAMS)
            for g in range(NG + 1):
                if g < NG:
                    pe.wait_ge(normed, g + 1)
                    if g >= 2:
                        pe.wait_ge(stage2_made, g - 1)
                    for u in range(GT):
                        i = pe.transpose(p_turn[g % 2][:, u, :], stages[g % 2][:, u, :], ident[:, :])
                    i.then_inc(turned, 1)
                m = g - 1
                if m >= 0:
                    pe.wait_ge(stage2_made, m + 1)
                    if m >= 2:
                        pe.wait_ge(nodes_made, m - 1)
                    for u in range(GT):
                        i = pe.matmul(p_prod[m % 2][:, u, :], stages2[m % 2][:, u, :], wn1a[:, :], start=True, stop=True)
                    i.then_inc(prod_made, 1)

            pe.wait_ge(sweeps_made, 1)
            sweeps, start, total, bodies = load_params(pe)
            hot_f = hot[:, :, :, :].bitcast(F32)
            def weight_product(u, q):
                pe.matmul(p_z, wt9[:, :], ew_s[:, u, q, :], start=True, stop=True).then_inc(z_done, 1)

            def hidden_product(u, q):
                k = slice(q * K_EDGE, (q + 1) * K_EDGE)
                pe.matmul(p_hid[q], we1[k, :], ea_s[k, u, :], start=True, stop=True).then_inc(hid_mm, 1)

            def edge_product(q, n):
                pe.wait_ge(hid_made, n)
                pe.matmul(p_ef[q], we2[:, :], hid[:, q, :], start=True, stop=True).then_inc(ef_mm, 1)

            def message_product(q, n):
                pe.wait_ge(ef_made, n)
                for t in range(TB):
                    i = pe.matmul(p_pre[q][:, t * D:(t + 1) * D], ef[:, q, t * P:(t + 1) * P], wn1b[:, :],
                                  start=True, stop=True)
                i.then_inc(pre_mm, 1)

            def aggregate(n):
                pe.wait_ge(msg_made, n)
                pe.wait_ge(hot_made, n)
                for q in (0, 1):
                    for t in range(TB):
                        pe.matmul(p_agg[:, q, 0, :], msg[:, q, t, :], hot_f[:, q, t, :],
                                  start=(t == 0), stop=(t == TB - 1))
                    for t in range(TB):
                        i = pe.matmul(p_agg[0:1, q, 1, :], ones[:, :], hot[:, q, t, :],
                                      start=(t == 0), stop=(t == TB - 1))
                i.then_inc(agg_mm, 1)

            def pair_step(b, u, first):
                n = b * (2 * RING) + 2 * u
                pe.wait_ge(in_loaded[u], b * 32 + 32)
                weight_product(u, 0)
                hidden_product(u, 0)
                hidden_product(u, 1)
                edge_product(0, n + 1)
                pe.wait_ge(tw_made, n + 1)
                weight_product(u, 1)
                edge_product(1, n + 2)
                if not first:
                    aggregate(n)
                message_product(0, n + 1)
                message_product(1, n + 2)

            pe.wait_ge(wt_placed, 16 * NP3)
            pe.wait_ge(nodes_made, NG)
            for u in range(RING):
                pair_step(0, u, u == 0)
            with pe.Fori(1, sweeps * NBODY) as b:
                for u in range(RING):
                    pair_step(b, u, False)
            aggregate(sweeps * NB)

            for g in range(NG):
                pe.wait_ge(acc_staged, g + 1)
                if g >= 2:
                    pe.wait_ge(x1_made, g - 1)
                for u in range(GT):
                    i = pe.matmul(p_prod[g % 2][:, u, :], stages[g % 2][:, u, :], wn2[:, :], start=True, stop=True)
                i.then_inc(upd_mm, 1)

            for g in range(NG):
                pe.wait_ge(staged1, g + 1)
                if g >= 2:
                    pe.wait_ge(acc1_made, g - 1)
                for u in range(GT):
                    i = pe.transpose(p_turn[g % 2][:, u, :], (stages2[0], stages[0])[g % 2][:, u, :], ident[:, :])
                i.then_inc(turned1, 1)
            pe.wait_ge(acc1_made, NG)

            pe.sem_inc(slot1_free, RING)
            pe.sem_inc(c_done, 1)
            pe.sem_inc(c_staged, 1)

            def sum_rows(b, u):
                n = b * (2 * RING) + 2 * u
                pe.wait_ge(hot1_made, n + 2)
                for q in (0, 1):
                    pe.wait_ge(gathered1[u][q], b * (16 * TB) + 16 * TB)
                    for t in range(TB):
                        for p in range(NP3):
                            i = pe.matmul(p_agg[:, q, 0, :], rows1[:, u, q, t, p, :], hot1[:, q, t, :],
                                          start=(t == 0 and p == 0), stop=(t == TB - 1 and p == NP3 - 1))
                i.then_inc(slot1_free, 1)

            seen = pe.alloc_register("seen")
            pe.reg_mov(seen, 0)

            def count_window(k, half, i):
                entry = pe.value_load(win_row[0:1, bass.ds(k + i * NCB, 1)], min_val=0, max_val=VISIT * (NTILE + 1) - 1)
                visits = nc.s_assert_within((entry // VISIT + (VTS[i] - 1)) // VTS[i], 1, MAX_VISITS,
                                            skip_runtime_bounds_check_because="the entry's form")
                pe.wait_ge(c_moved, k * CB + i + 1)
                pe.matmul(p_c[(half * CB + i) % 2], zeros[:, 0:P], zeros[:, :], start=True, stop=False, skip_group_check=True)
                with pe.Fori(0, visits):
                    used = pe.snap(seen, min_val=0, max_val=NWIN * MAX_VISITS * 2)
                    for h in (0, 1):
                        pe.wait_ge(c_hot, used + (h + 1))
                        for t in range(h * VH, h * VH + VTS[i] // 2):
                            m = pe.matmul(p_c[(half * CB + i) % 2], hot_src[:, t, :], hot_key[:, t, :], start=False, stop=True,
                                          skip_group_check=True)
                        m.then_inc(c_hot_free, 1)
                    pe.reg_add(seen, seen, 2)
                pe.matmul(p_c[(half * CB + i) % 2], zeros[:, 0:P], zeros[:, :], start=False, stop=True, skip_group_check=True)\
                  .then_inc(c_built, 1)

            cuts = [NT * i // (CB - 1) for i in range(CB)]

            def row_sums(batches, half, i):
                if i == 0:
                    pe.wait_ge(c_moved, batches * CB + 2)
                    pe.wait_ge(c_staged, batches)
                for a in range(cuts[i], cuts[i + 1]):
                    m = pe.matmul(p_cs, c_sums[half][:, a, :], nodes[:, a, :], start=(a == 0), stop=(a == NT - 1))
                if i == CB - 2:
                    m.then_inc(c_done, 1)

            def turn_rows(batches):
                pe.wait_ge(c_staged, batches + 1)
                pe.wait_ge(c_added, batches)
                pe.sem_inc(turns_begun, 1)
                pe.transpose(p_cst, c_rows[:, :], ident[0:CROW, 0:CROW]).then_inc(c_turned, 1)

            pe.wait_ge(win_loaded, 16)
            pe.wait_ge(normed1, NG)

            def batch(k, half, first):
                for i in range(CB):
                    if i < RING:
                        sum_rows(k, i)
                    if i == CB - 1 and not first:
                        turn_rows(k)
                    count_window(k, half, i)
                    if i < CB - 1 and not first:
                        row_sums(k, 1 - half, i)

            batch(0, 0, True)
            with pe.Fori(0, (NCB - 2) // 2) as kk:
                for j in (0, 1):
                    batch(kk * 2 + (1 + j), (1 + j) % 2, False)
            batch(NCB - 1, (NCB - 1) % 2, False)
            for i in range(CB - 1):
                row_sums(NCB, (NCB - 1) % 2, i)
            turn_rows(NCB)
            with pe.Fori(NCB, total) as b:
                for u in range(RING):
                    sum_rows(b, u)

            pe.wait_ge(acc1_added, total * (2 * RING))
            for g in range(NG + 1):
                if g < NG:
                    h = acc_group(g)
                    if g >= 2:
                        pe.wait_ge(hid2_made, g - 1)
                    pe.matmul(p_turn[g % 2][:, 0:4, :], w1[:, :], h[:, 0:4, :], start=True, stop=True)
                    pe.matmul(p_turn[g % 2][:, 4:GT, :], w1[:, :], h[:, 4:GT, :], start=True, stop=True)\
                      .then_inc(hid2_mm, 1)
                m = g - 1
                if m >= 0:
                    pe.wait_ge(hid2_made, m + 1)
                    if m >= 2:
                        pe.wait_ge(out_made, m - 1)
                    for u in range(GT):
                        i = pe.matmul(p_prod[m % 2][:, u, :], stages[m % 2][:, u, :], w2[:, :], start=True, stop=True)
                    i.then_inc(out_mm, 1)

        @block.vector
        def _(dve):
            step = [0]

            def chain(instruction):
                step[0] += 1
                return instruction.then_inc(dve_chain, 1)

            def settle():
                dve.wait_ge(dve_chain, step[0])

            chain(dve.memset(stats[:, :, :], 0.0))

            dve.wait_ge(dst_loaded, 16)
            by_tile = dst_b.rearrange("p j (t c) -> p j t c", t=TB)
            chain(dve.tensor_reduce(tleast[:, :, :], by_tile, AX.X, ALU.min))
            chain(dve.tensor_reduce(tgreat[:, :, :], by_tile, AX.X, ALU.max))
            settle()
            chain(dve.tensor_reduce(least[:, :], tleast[:, :, :], AX.X, ALU.min))
            dve.tensor_reduce(great[:, :], tgreat[:, :, :], AX.X, ALU.max).then_inc(base_made, 2)

            def layer_norm_scales(which):
                m_even, s_even, m_odd, s_odd = (stats[:, :, i] for i in (1, 2, 4, 5))
                chain(dve.tensor_tensor(mean[:, :], m_even, m_odd, ALU.add))
                chain(dve.tensor_tensor(half[:, :], m_even, m_odd, ALU.subtract))
                chain(dve.tensor_tensor(var[:, :], s_even, s_odd, ALU.add))
                settle()
                chain(dve.tensor_scalar(mean[:, :], mean[:, :], 0.5, None, ALU.mult))
                chain(dve.tensor_scalar(half[:, :], half[:, :], 0.5, None, ALU.mult))
                settle()
                chain(dve.tensor_tensor(half[:, :], half[:, :], half[:, :], ALU.mult))
                settle()
                chain(dve.scalar_tensor_tensor(out=var[:, :], in0=var[:, :], scalar=1.0 / D, in1=half[:, :],
                                               op0=ALU.mult, op1=ALU.add))
                settle()
                dve.tensor_scalar(var[:, :], var[:, :], EPS, None, ALU.add).then_inc(var_made, 1)
                dve.wait_ge(root_made, which)
                chain(dve.reciprocal(rstd[:, :], var[:, :]))
                settle()
                dve.scalar_tensor_tensor(out=shift[:, :], in0=mean[:, :], scalar=-1.0, in1=rstd[:, :],
                                         op0=ALU.mult, op1=ALU.mult).then_inc(stats_made, 1)

            for g in range(NG):
                dve.wait_ge(x_loaded[g], 16)
                for t in range(g * GT, (g + 1) * GT):
                    i = dve.bn_stats(stats[:, t, :], xs[:, t, :])
            chain(i)
            settle()
            layer_norm_scales(1)

            dve.wait_ge(base_loaded, 32)
            dve.wait_ge(consts_made, 10)
            chain(dve.tensor_tensor(span_row, great_all[0:1, :], base_all[0:1, :], ALU.subtract))
            chain(dve.tensor_scalar(cand_row, great_all[0:1, :], float(C_NODES), 1024.0, ALU.is_lt, ALU.mult))
            settle()
            chain(dve.tensor_tensor(cand_row, cand_row, blk_up[0:1, :], ALU.add))
            chain(dve.tensor_reduce(params[:, 0:1], span_row, AX.X, ALU.max))
            settle()
            chain(dve.tensor_scalar(cand_row, cand_row, 1.0, None, ALU.subtract))
            chain(dve.tensor_scalar(params[:, 0:1], params[:, 0:1], W_LOG2, None, ALU.logical_shift_right))
            settle()
            chain(dve.tensor_reduce(params[:, 1:2], cand_row, AX.X, ALU.min))
            chain(dve.tensor_scalar(params[:, 0:1], params[:, 0:1], 1, None, ALU.add))
            settle()
            chain(dve.tensor_scalar(params[:, 1:2], params[:, 1:2], 3, None, ALU.logical_shift_right))
            settle()
            chain(dve.tensor_scalar(params[:, 1:2], params[:, 1:2], NBODY - NCB - 1, None, ALU.min))
            settle()
            chain(dve.tensor_scalar(params[:, 3:4], params[:, 1:2], -1, NBODY, ALU.mult, ALU.add))
            settle()
            dve.tensor_tensor(params[:, 2:3], params[:, 3:4], params[:, 0:1], ALU.mult).then_inc(sweeps_made, 1)

            dve.wait_ge(params_loaded, 16 * N_PARAMS)
            bn1_g = bn1_r[:, :].rearrange("p (a d) -> p a d", a=1).to_broadcast([P, GT, D])
            for g in range(NG + 1):
                if g < NG:
                    x_g = xs[:, g * GT:(g + 1) * GT, :]
                    dve.wait_ge(normed, g + 1)
                    dve.tensor_tensor(x_g, x_g, stages[g % 2], ALU.add).then_inc(xh_made, 1)
                    dve.wait_ge(turned, g + 1)
                    if g >= 2:
                        dve.wait_ge(prod_made, g - 1)
                    dve.tensor_copy(stages2[g % 2], p_turn[g % 2]).then_inc(stage2_made, 1)
                m = g - 1
                if m >= 0:
                    dve.wait_ge(prod_made, m + 1)
                    dve.tensor_tensor(nodes[:, m * GT:(m + 1) * GT, :], p_prod[m % 2], bn1_g, ALU.add)\
                       .then_inc(nodes_made, 1)

            dve.wait_ge(sweeps_made, 1)
            sweeps, start, total, bodies = load_params(dve)

            dve.wait_ge(nodes_made, NG)
            chain(dve.tensor_copy(p_iota, iota_s[:, :]))

            def first_windows():
                chain(dve.tensor_copy(base_now[:, :], base_all[0:1, :]))
                chain(dve.tensor_tensor(rel[:, :].rearrange("p (n t) -> p n t", t=TB),
                                        dst_t[:, :].rearrange("p (n t) -> p n t", t=TB),
                                        base_all[:, :].rearrange("p (n a) -> p n a", a=1).to_broadcast([P, NB, TB]),
                                        ALU.subtract))
                settle()
                chain(dve.memset(rel[:, FULL_TILES + (TAIL > 0):NTILE], -float(2 * N_PAD)))
                if TAIL:
                    chain(dve.memset(rel[TAIL:P, FULL_TILES:FULL_TILES + 1], -float(2 * N_PAD)))
                settle()

            def next_windows(done, n):
                dve.tensor_scalar(rel[:, :], rel[:, :], float(W), None, ALU.subtract).then_inc(done, 1)
                dve.tensor_scalar(base_now[:, :], base_now[:, :], W, N_PAD, ALU.add, ALU.min).then_inc(done, 1)
                dve.wait_ge(done, n * 2 + 2)
                dve.sem_inc(windows_moved, 1)

            iota_t = p_iota.rearrange("p (a w) -> p a w", a=1).to_broadcast([P, TB, W])

            def one_hot(to, b, u, q):
                at = b * (RING * 2 * TB) + (2 * u + q) * TB
                r = rel[:, bass.ds(at, TB)].rearrange("p (t a) -> p t a", a=1).to_broadcast([P, TB, W])
                return dve.tensor_tensor(to[:, q, :, :], iota_t, r, ALU.is_equal)

            dve.wait_ge(dst_tiles_loaded, 16)
            first_windows()
            dve.sem_inc(slot_free, RING)

            dve.wait_ge(acc_zeroed, 1)
            chain(dve.memset(p_agg, 0.0))

            def window_base(blk):
                return dve.value_load(base_now[0:1, bass.ds(blk, 1)], min_val=0, max_val=N_PAD)

            def add_sums(total, blk, pairs):
                starts = [window_base(blk + q) for q in (0, 1)]
                dve.wait_ge(agg_mm, pairs)
                for q, at in enumerate(starts):
                    to = acc[:, :, bass.ds(at, W)]
                    dve.wait_ge(acc_added, total + q)
                    dve.tensor_tensor(to, p_agg[:, q, :, :], to, ALU.add).then_inc(acc_added, 1)

            def pair_step(s, b, u, first):
                total = s * NB + b * (2 * RING) + 2 * u
                for q in (0, 1):
                    dve.wait_ge(ef_mm, total + q + 1)
                    dve.wait_ge(tw_made, total + q + 1)
                    dve.scalar_tensor_tensor(out=ef[:, q, :], in0=p_ef[q], scalar=be2_c, in1=tw[:, q, :],
                                             op0=ALU.add, op1=ALU.mult).then_inc(ef_made, 1)
                if not first:
                    add_sums(total - 2, b * (2 * RING) + 2 * u - 2, s * NPAIR + b * RING + u)
                for q in (0, 1):
                    one_hot(hot, b, u, q).then_inc(hot_made, 1)
                for q in (0, 1):
                    dve.wait_ge(pre_mm, total + q + 1)
                    dve.wait_ge(gathered[u][q], (s * NBODY + b) * (16 * TB) + 16 * TB)
                    dve.tensor_tensor(msg[:, q, :, :].rearrange("p t d -> p (t d)"), p_pre[q],
                                      rows[:, u, q, :, :].rearrange("p t d -> p (t d)"), ALU.add)\
                       .then_inc(pre_made, 1)
                dve.wait_ge(pre_made, total + 2)
                dve.sem_inc(slot_free, 1)

            def window_entries(h):
                w = slice(0, NH)
                low, high, first, last, n = (win_n[w, i:i + 1] for i in range(5))
                chain(dve.tensor_scalar(low, win_low[w, :], float(h * NH * CW), None, ALU.add))
                chain(dve.tensor_scalar(high, win_low[w, :], float(h * NH * CW + CW - 1), None, ALU.add))
                settle()
                chain(dve.tensor_scalar(meets[w, :], tleast_all[w, :], high, None, ALU.is_le))
                settle()
                chain(dve.scalar_tensor_tensor(out=meets[w, :], in0=tgreat_all[w, :], scalar=low, in1=meets[w, :],
                                               op0=ALU.is_ge, op1=ALU.mult))
                settle()
                chain(dve.scalar_tensor_tensor(out=firsts[w, :], in0=tile_up[w, :], scalar=-float(NTILE + 1), in1=meets[w, :],
                                               op0=ALU.add, op1=ALU.mult))
                settle()
                chain(dve.tensor_reduce(first, firsts[w, :], AX.X, ALU.min))
                chain(dve.tensor_tensor(meets[w, :], meets[w, :], tile_up[w, :], ALU.mult))
                settle()
                chain(dve.tensor_reduce(last, meets[w, :], AX.X, ALU.max))
                chain(dve.tensor_scalar(first, first, float(NTILE), None, ALU.add))
                settle()
                chain(dve.tensor_scalar(first, first, float(NTILE - 1), None, ALU.min))
                settle()
                chain(dve.tensor_tensor(n, last, first, ALU.subtract))
                settle()
                chain(dve.tensor_scalar(n, n, 1.0, float(VISIT), ALU.max, ALU.mult))
                settle()
                dve.tensor_tensor(win_i[w, h:h + 1], n, first, ALU.add).then_inc(win_made, 1)

            def sweep(s, entries):
                for u in range(RING):
                    pair_step(s, 0, u, u == 0)
                    if entries and u % 2:
                        window_entries(u // 2)
                with dve.Fori(1, NBODY) as b:
                    for u in range(RING):
                        pair_step(s, b, u, False)
                add_sums(s * NB + NB - 2, NB - 2, s * NPAIR + NPAIR)
                dve.wait_ge(acc_added, s * NB + NB)
                next_windows(rel_made, s)

            dve.wait_ge(tile_ends_loaded, 32)
            dve.wait_ge(tile_up_made, 1)
            sweep(0, True)
            with dve.If(sweeps > 1):
                with dve.Fori(1, sweeps) as s:
                    sweep(s, False)

            dve.wait_ge(counts_moved, 16)

            def add_bias(g):
                for t in range(g * GT, (g + 1) * GT):
                    i = dve.scalar_tensor_tensor(out=xs[:, t, :], in0=bn2_r[:, :], scalar=count_n[:, t:t + 1],
                                                 in1=xs[:, t, :], op0=ALU.mult, op1=ALU.add)
                i.then_inc(x1_chain, 1)

            add_bias(0)
            for g in range(NG):
                x_g = xs[:, g * GT:(g + 1) * GT, :]
                dve.wait_ge(upd_mm, g + 1)
                dve.wait_ge(x1_chain, g + 1)
                dve.tensor_tensor(x_g, x_g, p_prod[g % 2], ALU.add).then_inc(x1_made, 1)
                if g < NG - 1:
                    add_bias(g + 1)
                dve.wait_ge(x1_made, g + 1)
                for t in range(g * GT, (g + 1) * GT):
                    i = dve.bn_stats(stats[:, t, :], xs[:, t, :])
                i.then_inc(x1_stats, 1)
            dve.wait_ge(x1_stats, NG)
            layer_norm_scales(2)

            for g in range(NG):
                dve.wait_ge(parts_first, g + 1)
                if g:
                    dve.wait_ge(parts_made, g)
                dve.tensor_tensor(left, nodes[:, g * GT:(g + 1) * GT, :], parts[:, g % 2, :, 0, :], ALU.subtract)\
                   .then_inc(parts_chain, 1)
                dve.wait_ge(parts_chain, 2 * g + 1)
                dve.tensor_copy(parts[:, g % 2, :, 1, :], left).then_inc(parts_chain, 1)
                dve.wait_ge(parts_chain, 2 * g + 2)
                dve.tensor_tensor(parts[:, g % 2, :, 2, :], left, parts[:, g % 2, :, 1, :], ALU.subtract)\
                   .then_inc(parts_made, 1)
                dve.wait_ge(turned1, g + 1)
                dve.tensor_copy(acc_group(g), p_turn[g % 2]).then_inc(acc1_made, 1)
            first_windows()
            chain(dve.tensor_copy(p_iota, iota_s[:, :]))
            settle()
            dve.wait_ge(acc1_made, NG)

            def add_sums1(batches, total, blk, pairs):
                starts = [window_base(blk + q) for q in (0, 1)]
                dve.wait_ge(c_added, batches)
                dve.wait_ge(slot1_free, pairs + RING)
                for q, at in enumerate(starts):
                    to = acc[:, 0, bass.ds(at, W)]
                    dve.wait_ge(acc1_added, total + q)
                    dve.tensor_tensor(to, p_agg[:, q, 0, :], to, ALU.add).then_inc(acc1_added, 1)

            def pair_hots(b, u):
                for q in (0, 1):
                    one_hot(hot1, b, u, q).then_inc(hot1_made, 1)

            def pair_sums(n, b, u, batches):
                add_sums1(batches, n * (2 * RING) + 2 * u, b * (2 * RING) + 2 * u, n * RING + u + 1)

            dve.wait_ge(src_loaded, 16)
            chain(dve.tensor_scalar(src_b, src_i, 1.0 / NT, 0.5 / NT - 0.5, ALU.mult, ALU.add))
            settle()
            chain(dve.tensor_scalar(src_b, src_b, ROUND, None, ALU.add))
            settle()
            chain(dve.tensor_scalar(src_b, src_b, ROUND, None, ALU.subtract))
            settle()
            chain(dve.scalar_tensor_tensor(out=src_t, in0=src_b, scalar=-float(NT), in1=src_i,
                                           op0=ALU.mult, op1=ALU.add))
            settle()
            chain(dve.scalar_tensor_tensor(out=key, in0=dst_t[:, :], scalar=float(NT), in1=src_t,
                                           op0=ALU.mult, op1=ALU.add))
            settle()
            chain(dve.tensor_scalar(rel_add, dst_t[:, :], float(C_NODES), -float(2 * N_PAD), ALU.is_lt, ALU.mult))
            settle()
            chain(dve.tensor_tensor(rel[:, :], rel[:, :], rel_add, ALU.add))
            chain(dve.memset(key_all[:, FULL_TILES + (TAIL > 0):NTILE + VT], -1.0))
            chain(dve.memset(src_b_all[:, NTILE:NTILE + VT], 0.0))
            if TAIL:
                chain(dve.memset(key[TAIL:P, FULL_TILES:FULL_TILES + 1], -1.0))
            settle()

            seen = dve.alloc_register("seen")
            dve.reg_mov(seen, 0)

            iota_v = iota_b[:, :].rearrange("p (a c) -> p a c", a=1)

            def window_hots(k, i):
                win = k + i * NCB
                entry = dve.value_load(win_row[0:1, bass.ds(win, 1)], min_val=0, max_val=VISIT * (NTILE + 1) - 1)
                first = entry % VISIT
                visits = nc.s_assert_within((entry // VISIT + (VTS[i] - 1)) // VTS[i], 1, MAX_VISITS,
                                            skip_runtime_bounds_check_because="the entry's form")
                with dve.Fori(0, visits) as v:
                    at = nc.s_assert_within(first + v * VTS[i], 0, NTILE - 1,
                                            skip_runtime_bounds_check_because="the last visit begins at a tile")
                    made = dve.snap(seen, min_val=0, max_val=NWIN * MAX_VISITS * 2)
                    n = VTS[i] // 2
                    for h in (0, 1):
                        dve.wait_ge(c_hot_free, made + (h + 1))
                        half_src = src_b_all[:, h * n:NTILE + VT][:, bass.ds(at, n)].rearrange("p (t a) -> p t a", a=1)
                        dve.tensor_tensor(hot_src[:, h * VH:h * VH + n, :], iota_v.to_broadcast([P, n, P]),
                                          half_src.to_broadcast([P, n, P]), ALU.is_equal)
                        for t in range(n):
                            m = dve.tensor_scalar(hot_key[:, h * VH + t, :], iota_k[:, :], win_off[:, bass.ds(win, 1)],
                                                  key_all[:, h * n + t:NTILE + VT][:, bass.ds(at, 1)],
                                                  ALU.add, ALU.is_equal)
                        m.then_inc(c_hot, 1)
                    dve.reg_add(seen, seen, 2)

            dve.wait_ge(win_loaded, 16)
            dve.sem_inc(c_hot_free, 2)
            dve.sem_inc(c_moved, 2)
            dve.sem_inc(c_added, 1)
            acc_c = acc[:, 0, 0:C_NODES].rearrange("p (i k n) -> p k i n", k=NCB, n=CW)

            def add_rows(batches):
                dve.wait_ge(c_turned, batches)
                to = acc_c[:, bass.ds(batches - 1, 1), :, :].rearrange("p a i n -> p (a i) n")
                dve.tensor_tensor(to, p_cst.rearrange("p (i n) -> p i n", i=CB), to, ALU.add).then_inc(c_added, 1)

            def batch(k, first):
                at = body_at(start, k)
                for i in range(CB):
                    if i < RING:
                        pair_hots(at, i)
                    window_hots(k, i)
                    if i < RING:
                        pair_sums(k, at, i, 1 if first else k)
                if not first:
                    dve.wait_ge(acc1_added, k * (2 * RING) + 2 * RING)
                    add_rows(k)

            batch(0, True)
            with dve.Fori(1, NCB) as k:
                batch(k, False)
            dve.wait_ge(acc1_added, NCB * (2 * RING))
            add_rows(NCB)
            with dve.Fori(NCB, bodies) as b:
                for u in range(RING):
                    pair_hots(body_at(start, b), u)
                    pair_sums(b, body_at(start, b), u, NCB + 1)
            with dve.If(sweeps > 1):
                body = dve.alloc_register("body")
                dve.reg_mov(body, bodies)
                with dve.Fori(1, sweeps) as s:
                    done = dve.snap(body, min_val=0, max_val=MAX_SWEEPS * NBODY)
                    dve.wait_ge(acc1_added, done * (2 * RING))
                    next_windows(rel1_made, s - 1)
                    with dve.Fori(0, bodies) as b:
                        done = dve.snap(body, min_val=0, max_val=MAX_SWEEPS * NBODY)
                        for u in range(RING):
                            pair_hots(body_at(start, b), u)
                            pair_sums(done, body_at(start, b), u, NCB + 1)
                        dve.reg_add(body, body, 1)

            b2_g = b2_r[:, :].rearrange("p (a d) -> p a d", a=1).to_broadcast([P, GT, D])
            for g in range(NG):
                x_g, y = xs[:, g * GT:(g + 1) * GT, :], stages2[g % 2]
                dve.wait_ge(out_mm, g + 1)
                dve.tensor_tensor(y, p_prod[g % 2], b2_g, ALU.add).then_inc(out_chain, 1)
                dve.wait_ge(out_chain, g + 1)
                dve.scalar_tensor_tensor(out=x_g, in0=y, scalar=0.0, in1=x_g, op0=ALU.max, op1=ALU.add)\
                   .then_inc(out_made, 1)


def kernel(x, src, dst, edge_attr_64, edge_weight, **w):
    import numpy as np
    import concourse.bacc as bacc
    from concourse.bass_utils import run_bass_kernel_spmd

    x, src, dst, ea, ew = (np.asarray(a) for a in (x, src, dst, edge_attr_64, edge_weight))
    extra = E_PAD - N_EDGES
    src = np.pad(src, (0, extra))
    dst = np.pad(dst, (0, extra), mode="edge")
    ea = np.pad(ea, ((0, extra), (0, 0)))
    arrays = {
        "x": np.pad(x, ((0, N_PAD - N_NODES), (0, 0))).reshape(P, NT * D),
        "ea": ea.reshape(NPAIR, 2, BLK, K_EDGE).transpose(0, 1, 3, 2).reshape(NPAIR, P, BLK),
        "ew": np.pad(ew, (0, extra)).reshape(P, E_PAD // P),
        "src": src.reshape(NPAIR, 2 * TB, P).transpose(0, 2, 1),
        "src_tiles": src.reshape(NTILE, P).T,
        "dst_tiles": dst.reshape(NTILE, P).T,
        "dst_blocks": dst.reshape(NBP, NBJ, BLK),
    }
    names = {"We1": "L0_gnn_We1", "be1": "L0_gnn_be1", "We2": "L0_gnn_We2", "be2": "L0_gnn_be2", "Wt": "L0_gnn_Wt",
             "bt": "L0_gnn_bt", "Wn1": "L0_gnn_Wn1", "bn1": "L0_gnn_bn1", "Wn2": "L0_gnn_Wn2", "bn2": "L0_gnn_bn2",
             "W1": "L1_gnn_W1", "b1": "L1_gnn_b1", "W2": "L1_gnn_W2", "b2": "L1_gnn_b2"}
    for short, name in names.items():
        arrays[short] = np.asarray(w[name])
    arrays = {k: np.ascontiguousarray(a) for k, a in arrays.items()}
    nc = bacc.Bacc("TRN2", target_bir_lowering=False, num_devices=1)
    args = {k: nc.dram_tensor(f"in_{k}", a.shape, mybir.dt.from_np(a.dtype), kind="ExternalInput").ap()
            for k, a in arrays.items()}
    out = nc.dram_tensor("out", (P, NT * D), F32, kind="ExternalOutput").ap()
    gnn_program(nc, **args, out=out)
    r = run_bass_kernel_spmd(nc, [{f"in_{k}": a for k, a in arrays.items()}], core_ids=[0])
    return r.results[0]["out"].reshape(N_PAD, D)[:N_NODES]
```
